# Optimizing a Trainium2 kernel written in Bass

```python
import numpy as np
import jax
import jax.numpy as jnp

def _softmax(x, axis=-1):
    return jax.nn.softmax(x, axis=axis)

def _gelu(x):
    return jax.nn.gelu(x, approximate=True)

def _silu(x):
    return jax.nn.silu(x)

def _sigmoid(x):
    return jax.nn.sigmoid(x)

def _layernorm(x, axis=-1, eps=1e-05):
    m = jnp.mean(x, axis=axis, keepdims=True)
    v = jnp.var(x, axis=axis, keepdims=True)
    return (x - m) / jnp.sqrt(v + eps)

def _scatter_add(tgt, idx, src, axis=0):
    return tgt.at[idx].add(src)

def _segment_sum(src, seg, n):
    return jax.ops.segment_sum(src, seg, n)
kernel_name = 'mk_rec_standalone_d1_rec_r8_4391de'

def setup_inputs(seed: int=0):
    np.random.seed(seed)
    _w = jnp.asarray

    def _rec_inputs():
        import jax
        import jax.numpy as jnp
        _rk = jax.random.key(seed)
        r_dense = -0.00338568 + 1.0005 * jax.random.normal(jax.random.fold_in(_rk, 1), (2048, 13), jnp.float32)
        r_sparse = jnp.stack([jax.random.randint(jax.random.fold_in(jax.random.fold_in(_rk, 2), 0), (2048,), 2, 12500, jnp.int32), jax.random.randint(jax.random.fold_in(jax.random.fold_in(_rk, 2), 1), (2048,), 1, 99999, jnp.int32), jax.random.randint(jax.random.fold_in(jax.random.fold_in(_rk, 2), 2), (2048,), 0, 12500, jnp.int32), jax.random.randint(jax.random.fold_in(jax.random.fold_in(_rk, 2), 3), (2048,), 5, 12500, jnp.int32), jax.random.randint(jax.random.fold_in(jax.random.fold_in(_rk, 2), 4), (2048,), 20, 99993, jnp.int32), jax.random.randint(jax.random.fold_in(jax.random.fold_in(_rk, 2), 5), (2048,), 0, 99993, jnp.int32), jax.random.randint(jax.random.fold_in(jax.random.fold_in(_rk, 2), 6), (2048,), 2, 99999, jnp.int32), jax.random.randint(jax.random.fold_in(jax.random.fold_in(_rk, 2), 7), (2048,), 2, 99995, jnp.int32), jax.random.randint(jax.random.fold_in(jax.random.fold_in(_rk, 2), 8), (2048,), 0, 99999, jnp.int32), jax.random.randint(jax.random.fold_in(jax.random.fold_in(_rk, 2), 9), (2048,), 2, 99986, jnp.int32), jax.random.randint(jax.random.fold_in(jax.random.fold_in(_rk, 2), 10), (2048,), 4, 99999, jnp.int32), jax.random.randint(jax.random.fold_in(jax.random.fold_in(_rk, 2), 11), (2048,), 15, 99999, jnp.int32), jax.random.randint(jax.random.fold_in(jax.random.fold_in(_rk, 2), 12), (2048,), 0, 99989, jnp.int32), jax.random.randint(jax.random.fold_in(jax.random.fold_in(_rk, 2), 13), (2048,), 5, 99990, jnp.int32), jax.random.randint(jax.random.fold_in(jax.random.fold_in(_rk, 2), 14), (2048,), 2, 99996, jnp.int32), jax.random.randint(jax.random.fold_in(jax.random.fold_in(_rk, 2), 15), (2048,), 3, 99994, jnp.int32), jax.random.randint(jax.random.fold_in(jax.random.fold_in(_rk, 2), 16), (2048,), 0, 99998, jnp.int32), jax.random.randint(jax.random.fold_in(jax.random.fold_in(_rk, 2), 17), (2048,), 13, 99998, jnp.int32), jax.random.randint(jax.random.fold_in(jax.random.fold_in(_rk, 2), 18), (2048,), 10, 12498, jnp.int32), jax.random.randint(jax.random.fold_in(jax.random.fold_in(_rk, 2), 19), (2048,), 0, 99999, jnp.int32), jax.random.randint(jax.random.fold_in(jax.random.fold_in(_rk, 2), 20), (2048,), 0, 99995, jnp.int32), jax.random.randint(jax.random.fold_in(jax.random.fold_in(_rk, 2), 21), (2048,), 1, 99998, jnp.int32), jax.random.randint(jax.random.fold_in(jax.random.fold_in(_rk, 2), 22), (2048,), 1, 99997, jnp.int32), jax.random.randint(jax.random.fold_in(jax.random.fold_in(_rk, 2), 23), (2048,), 2, 99989, jnp.int32), jax.random.randint(jax.random.fold_in(jax.random.fold_in(_rk, 2), 24), (2048,), 6, 12500, jnp.int32), jax.random.randint(jax.random.fold_in(jax.random.fold_in(_rk, 2), 25), (2048,), 2, 99995, jnp.int32)], axis=1)
        return (r_dense, r_sparse)
    r_dense, r_sparse = _rec_inputs()

    def _L0_rec_setup():
        import jax, jax.numpy as jnp
        import numpy as np
        B = 2048
        NUM_DENSE = 13
        NUM_SPARSE = 26
        VOCAB = 12500
        DIM = 128
        BOTTOM = [512, 256, 128]
        TOP = [1024, 1024, 512, 256, 1]
        NUM_FEAT = 1 + NUM_SPARSE
        _TRIU = np.triu_indices(NUM_FEAT, k=1)

        def _linear_params(key, dims):
            Ws, bs = ([], [])
            for i, (din, dout) in enumerate(zip(dims[:-1], dims[1:])):
                k = jax.random.fold_in(key, i)
                Ws.append(jax.random.normal(k, (din, dout), dtype=jnp.float32) * (1.0 / np.sqrt(din)))
                bs.append(jnp.zeros((dout,), dtype=jnp.float32))
            return (Ws, bs)

        def _mlp(x, Ws, bs):
            for W, b in zip(Ws, bs):
                x = jax.nn.relu(x @ W + b)
            return x
        key = jax.random.key(seed)
        k_dense, k_sparse, k_emb, k_bot, k_top = jax.random.split(key, 5)
        dense = jax.random.normal(k_dense, (B, NUM_DENSE), dtype=jnp.float32)
        sparse = jax.random.randint(k_sparse, (B, NUM_SPARSE), 0, VOCAB, dtype=jnp.int64)
        emb_tables = jax.random.normal(k_emb, (NUM_SPARSE, VOCAB, DIM), dtype=jnp.float32) * 0.01
        bWs, bbs = _linear_params(k_bot, [NUM_DENSE] + BOTTOM)
        inter_dim = NUM_FEAT * (NUM_FEAT - 1) // 2 + BOTTOM[-1]
        tWs, tbs = _linear_params(k_top, [inter_dim] + TOP)
        return {'dense': dense, 'sparse': sparse, 'emb_tables': emb_tables, 'bw0': bWs[0], 'bb0': bbs[0], 'bw1': bWs[1], 'bb1': bbs[1], 'bw2': bWs[2], 'bb2': bbs[2], 'tw0': tWs[0], 'tb0': tbs[0], 'tw1': tWs[1], 'tb1': tbs[1], 'tw2': tWs[2], 'tb2': tbs[2], 'tw3': tWs[3], 'tb3': tbs[3], 'tw4': tWs[4], 'tb4': tbs[4]}
    _L0_rec_all = _L0_rec_setup()
    _L0_rec_in = {k: v for k, v in _L0_rec_all.items() if k in ('emb_tables', 'bw0', 'bb0', 'bw1', 'bb1', 'bw2', 'bb2', 'tw0', 'tb0', 'tw1', 'tb1', 'tw2', 'tb2', 'tw3', 'tb3', 'tw4', 'tb4')}
    del _L0_rec_all
    return {'r_dense': r_dense, 'r_sparse': r_sparse, 'L0_rec_emb_tables': _L0_rec_in['emb_tables'], 'L0_rec_bw0': _L0_rec_in['bw0'], 'L0_rec_bb0': _L0_rec_in['bb0'], 'L0_rec_bw1': _L0_rec_in['bw1'], 'L0_rec_bb1': _L0_rec_in['bb1'], 'L0_rec_bw2': _L0_rec_in['bw2'], 'L0_rec_bb2': _L0_rec_in['bb2'], 'L0_rec_tw0': _L0_rec_in['tw0'], 'L0_rec_tb0': _L0_rec_in['tb0'], 'L0_rec_tw1': _L0_rec_in['tw1'], 'L0_rec_tb1': _L0_rec_in['tb1'], 'L0_rec_tw2': _L0_rec_in['tw2'], 'L0_rec_tb2': _L0_rec_in['tb2'], 'L0_rec_tw3': _L0_rec_in['tw3'], 'L0_rec_tb3': _L0_rec_in['tb3'], 'L0_rec_tw4': _L0_rec_in['tw4'], 'L0_rec_tb4': _L0_rec_in['tb4']}

def reference(r_dense, r_sparse, L0_rec_emb_tables, L0_rec_bw0, L0_rec_bb0, L0_rec_bw1, L0_rec_bb1, L0_rec_bw2, L0_rec_bb2, L0_rec_tw0, L0_rec_tb0, L0_rec_tw1, L0_rec_tb1, L0_rec_tw2, L0_rec_tb2, L0_rec_tw3, L0_rec_tb3, L0_rec_tw4, L0_rec_tb4):
    import jax
    import jax.numpy as jnp

    def _L0_rec_ref(dense, sparse, emb_tables, bw0, bb0, bw1, bb1, bw2, bb2, tw0, tb0, tw1, tb1, tw2, tb2, tw3, tb3, tw4, tb4):
        import jax, jax.numpy as jnp
        import numpy as np
        B = 2048
        NUM_DENSE = 13
        NUM_SPARSE = 26
        VOCAB = 12500
        DIM = 128
        BOTTOM = [512, 256, 128]
        TOP = [1024, 1024, 512, 256, 1]
        NUM_FEAT = 1 + NUM_SPARSE
        _TRIU = np.triu_indices(NUM_FEAT, k=1)

        def _linear_params(key, dims):
            Ws, bs = ([], [])
            for i, (din, dout) in enumerate(zip(dims[:-1], dims[1:])):
                k = jax.random.fold_in(key, i)
                Ws.append(jax.random.normal(k, (din, dout), dtype=jnp.float32) * (1.0 / np.sqrt(din)))
                bs.append(jnp.zeros((dout,), dtype=jnp.float32))
            return (Ws, bs)

        def _mlp(x, Ws, bs):
            for W, b in zip(Ws, bs):
                x = jax.nn.relu(x @ W + b)
            return x
        dense_out = _mlp(dense, [bw0, bw1, bw2], [bb0, bb1, bb2])
        sparse_embeds = emb_tables[jnp.arange(NUM_SPARSE)[None, :], sparse]
        features = jnp.concatenate([dense_out[:, None, :], sparse_embeds], axis=1)
        inter = jnp.einsum('bnd,bmd->bnm', features, features)
        interacted = inter[:, _TRIU[0], _TRIU[1]]
        concat = jnp.concatenate([dense_out, interacted], axis=-1)
        out = _mlp(concat, [tw0, tw1, tw2, tw3, tw4], [tb0, tb1, tb2, tb3, tb4])
        return out.squeeze(-1)
    y = _L0_rec_ref(r_dense, r_sparse, L0_rec_emb_tables, L0_rec_bw0, L0_rec_bb0, L0_rec_bw1, L0_rec_bb1, L0_rec_bw2, L0_rec_bb2, L0_rec_tw0, L0_rec_tb0, L0_rec_tw1, L0_rec_tb1, L0_rec_tw2, L0_rec_tb2, L0_rec_tw3, L0_rec_tb3, L0_rec_tw4, L0_rec_tb4)
    return y

_drawn_inputs = setup_inputs


def setup_inputs(seed=0):
    import zlib

    import numpy as np

    out = dict(_drawn_inputs(seed))
    spreads = {'L0_rec_bb0': (0.0, 0.1),
     'L0_rec_bb1': (0.0, 0.1),
     'L0_rec_bb2': (0.0, 0.1),
     'L0_rec_tb0': (0.0, 0.1),
     'L0_rec_tb1': (0.0, 0.1),
     'L0_rec_tb2': (0.0, 0.1),
     'L0_rec_tb3': (0.0, 0.1)}
    factors = {}
    for name, (base, spread) in spreads.items():
        noise = np.random.default_rng([zlib.crc32(name.encode()), seed]).standard_normal(out[name].shape)
        drawn = base * np.exp(spread * noise) if base else spread * noise
        out[name] = jnp.asarray(drawn.astype(out[name].dtype))
    for name, factor in factors.items():
        out[name] = (out[name] * factor).astype(out[name].dtype)
    return out
```

```python
from contextlib import ExitStack

import concourse.bass as bass
from concourse import mybir
from concourse.alu_op_type import AluOpType as ALU

F32 = mybir.dt.float32
F32R = mybir.dt.float32r
I32 = mybir.dt.int32
ACT = mybir.ActivationFunctionType
AX = mybir.AxisListType

P = 128


def dlrm(nc, dense, sparse, emb, bw0, bb0, bw1, bb1, bw2, bb2,
         tw0, tb0, tw1, tb1, tw2, tb2, tw3, tb3, tw4, tb4, out):
    B, ND = dense.shape
    NT, V, D = emb.shape
    NF = NT + 1
    H0, H1 = bw0.shape[1], bw1.shape[1]
    M0, M1, M2, M3 = tw0.shape[1], tw1.shape[1], tw2.shape[1], tw3.shape[1]
    PAIRS = NF * (NF - 1) // 2
    C = 256
    HALF = C // 2
    BS = C // 4
    TILES = B // C
    BLOCKS = B // BS
    SL = NT // 2
    TG = 4
    QT = -(-SL // TG)
    SG = 4
    NN = NF - 1
    NP = 32
    GG = 4
    QG = BS // SG // GG
    QB = QT + QG
    KX = 1 + -(-PAIRS // P)
    LAST = PAIRS - (KX - 2) * P
    O0, O1, O2, O3 = M0 // P, M1 // P, M2 // P, M3 // P
    B0, B1 = H0 // P, H1 // P
    EV = O0 + O1 + O2 + O3
    BEV = B0 + B1 + 1
    RA, RB = 3, 3
    assert (D, NT, C, BS, QT, QG, O0, O1, O2, O3, B0, B1, KX) == (P, 26, 256, 64, 4, 4, 8, 8, 4, 2, 4, 2, 4)

    runs = []
    row = 0
    for n in range(NN):
        m, left = n + 1, NN - n
        while left:
            take = min(left, P - row % P)
            runs.append((n, m, row // P, row % P, take))
            row, m, left = row + take, m + take, left - take
    PAIR_DMA = 16 * len(runs)

    table_rows = emb.rearrange("t v d -> (t v) d")
    dense_hi = nc.dram_tensor("dense_hi", (P, B), F32, kind="Internal").ap()
    dense_lo = nc.dram_tensor("dense_lo", (P, B), F32, kind="Internal").ap()

    with ExitStack() as ctx:
        def sb(name, shape, dt):
            return ctx.enter_context(nc.sbuf_tensor(name, shape, dt))

        def sem(name):
            return ctx.enter_context(nc.semaphore(name))

        w01_hi = sb("w01_hi", [P, KX + O0, M0], F32R)
        w01_lo = sb("w01_lo", [P, KX + O0, M0], F32R)
        w3_hi = sb("w3_hi", [P, O2, M3], F32R)
        w3_lo = sb("w3_lo", [P, O2, M3], F32R)
        ringA_hi = sb("ringA_hi", [P, RA, C], F32R)
        ringA_lo = sb("ringA_lo", [P, RA, C], F32R)
        ringB_hi = sb("ringB_hi", [P, RB, C], F32R)
        ringB_lo = sb("ringB_lo", [P, RB, C], F32R)
        pair_rows = sb("pair_rows", [P, KX - 1, C], F32)
        act_f32 = sb("act_f32", [P, 2, C], F32)
        feat_hi = sb("feat_hi", [P, BS, NP], F32R)
        feat_lo = sb("feat_lo", [P, BS, NP], F32R)
        feat0 = sb("feat0", [P, 2, BS], F32)
        rows = [sb(f"rows{i}", [P, SL, D], F32) for i in range(2)]
        gram = sb("gram", [P, NN, HALF], F32)
        idx_all = sb("idx_all", [P, BLOCKS + 1, SL], I32)
        idx_cur = sb("idx_cur", [P, 4, SL], I32)
        ident = sb("ident", [P, P], F32)
        bias = sb("bias", [P, 32], F32)
        w4 = sb("w4", [P, O3, 2], F32R)
        b4 = sb("b4", [P, 1], F32)
        z = sb("z", [P, 2], F32)
        z_all = sb("z_all", [P, B // P], F32)

        with nc.sbuf_tensor("stage", [P, 2, M0], F32) as stage:
            pass
        x_hi = sb("x_hi", [P, KX, C], F32R)
        x_lo = sb("x_lo", [P, KX, C], F32R)
        with ExitStack() as early:
            dense_T = early.enter_context(nc.sbuf_tensor("dense_T", [96, B], F32R))
            bw0s = early.enter_context(nc.sbuf_tensor("bw0s", [96, H0], F32R))
            bw1_hi = early.enter_context(nc.sbuf_tensor("bw1_hi", [P, B0, H1], F32R))
            bw1_lo = early.enter_context(nc.sbuf_tensor("bw1_lo", [P, B0, H1], F32R))
            bw2_hi = early.enter_context(nc.sbuf_tensor("bw2_hi", [P, B1, D], F32R))
            bw2_lo = early.enter_context(nc.sbuf_tensor("bw2_lo", [P, B1, D], F32R))
            dense_rows = early.enter_context(nc.sbuf_tensor("dense_rows", [P, B // P, ND], F32))
            table_base = early.enter_context(nc.sbuf_tensor("table_base", [P, NT], I32))
            bot0_hi = early.enter_context(nc.sbuf_tensor("bot0_hi", [P, B0, C], F32R))
            bot0_lo = early.enter_context(nc.sbuf_tensor("bot0_lo", [P, B0, C], F32R))
            vec_rows = early.enter_context(nc.sbuf_tensor("vec_rows", [32, P], F32))
        w2_hi = sb("w2_hi", [P, O1, M2], F32R)
        w2_lo = sb("w2_lo", [P, O1, M2], F32R)

        WI = BLOCKS * NT
        gram_flat = gram[:, :, :].rearrange("p m b -> p (m b)")
        raw_idx = gram_flat[:, 0:WI].bitcast(I32).rearrange("p (k t) -> p k t", t=NT)
        wrap = gram_flat[:, WI:2 * WI].rearrange("p (k t) -> p k t", t=NT)
        wrapped = gram_flat[:, 2 * WI:3 * WI].rearrange("p (k t) -> p k t", t=NT)
        clamped = gram_flat[:, 3 * WI:4 * WI].rearrange("p (k t) -> p k t", t=NT)

        bank = [ctx.enter_context(nc.psum_tensor(f"bank{i}", [P, 512], F32)) for i in range(8)]

        s_idx = [sem("idx_first"), sem("idx_rest")]
        s_vec = sem("vectors_loaded")
        s_b4 = sem("b4_loaded")
        s_dense = sem("dense_loaded")
        s_stage = [sem("stage0_loaded"), sem("stage1_loaded")]
        s_rows = [sem("rows0_gathered"), sem("rows1_gathered")]
        s_scratch = sem("dense_out_stored")
        s_feat0 = sem("feature0_loaded")
        s_pairs = [sem("pairs_half0_moved"), sem("pairs_half1_moved")]
        s_x0 = sem("x_dense_loaded")
        s_out = sem("out_stored")
        g_const = sem("constants_made")
        g_block = sem("gather_begun")
        p_pre = sem("pe_prologue_transposes")
        p_bot = sem("pe_bottom")
        p_tr = sem("pe_transposed")
        p_gr = sem("pe_gram")
        p_l0, p_k1, p_l1, p_k2, p_l2, p_l3, p_l4 = (sem("pe_layer0"), sem("pe_layer1_step"), sem("pe_layer1"),
                                                   sem("pe_layer2_step"), sem("pe_layer2"), sem("pe_layer3"),
                                                   sem("pe_layer4"))
        p_z = sem("pe_out_transposed")
        a_split, v_split = sem("act_weights_hi"), sem("vec_weights_lo")
        a_pre, v_pre = sem("act_dense_hi"), sem("vec_dense_lo")
        a_tr, v_tr = sem("act_features_hi"), sem("vec_features_lo")
        a_gr, v_gr = sem("act_gram"), sem("vec_gram")
        a_ev, v_ev = sem("act_layer_hi"), sem("vec_layer_lo")
        a_x, v_x = sem("act_x_hi"), sem("vec_x_lo")
        v_zero = sem("vec_zeroed")
        v_i = sem("vec_index_steps")
        v_idx0 = sem("vec_first_indices")
        v_idx = sem("vec_indices_refreshed")
        v_bias = sem("vec_bias")
        v_w4 = sem("vec_w4")
        v_zs, v_z, v_zt = sem("vec_z_sum"), sem("vec_z"), sem("vec_z_transposed")

        c_bb0, c_bb1, c_bb2 = 0, B0, B0 + B1
        c_t0 = c_bb2 + 1
        c_t1, c_t2, c_t3 = c_t0 + O0, c_t0 + O0 + O1, c_t0 + O0 + O1 + O2
        c_w4 = c_t3 + O3
        vectors = [(bb0, c_bb0, B0), (bb1, c_bb1, B1), (bb2, c_bb2, 1), (tb0, c_t0, O0), (tb1, c_t1, O1),
                   (tb2, c_t2, O2), (tb3, c_t3, O3)]
        N_VEC = c_w4 + O3

        def rhs_of(feat, g):
            return feat[:, SG * g:SG * g + SG, 1:NF]

        def lhs_of(feat, g):
            return feat[:, SG * g:SG * g + SG, :].rearrange("p s n -> p (s n)")

        def piece_bank(q):
            return bank[6 + q % 2]

        def half_bank(first, k):
            return bank[first + k // 2][:, C * (k % 2):C * (k % 2) + C]

        def bottom_tile(o):
            if o < B0:
                return half_bank(0, o), bot0_hi[:, o, :], bot0_lo[:, o, :]
            k = o - B0
            return half_bank(2, k) if k < B1 else bank[3][:, 0:C], ringB_hi[:, k, :], ringB_lo[:, k, :]

        def h0_tile(k):
            return bank[4 + k % 2][:, 0:C], ringA_hi[:, k % RA, :], ringA_lo[:, k % RA, :]

        def h1_tile(k):
            return half_bank(0, k), ringB_hi[:, k % RB, :], ringB_lo[:, k % RB, :]

        def h2_tile(k):
            if k < RA:
                return half_bank(4, k), ringA_hi[:, k, :], ringA_lo[:, k, :]
            return half_bank(4, k), ringB_hi[:, RB - 1, :], ringB_lo[:, RB - 1, :]

        def h3_tile(k):
            return half_bank(0, k), ringB_hi[:, k, :], ringB_lo[:, k, :]

        EV0 = BEV * TILES

        def tr_cols(q):
            return (min(SL, TG * (q + 1)) - TG * q) * P

        def transposed(ps, q):
            return ps[:, 0:tr_cols(q)].rearrange("p (f b) -> p f b", b=BS)

        def feat_of(feat, q):
            f = 1 + 2 * TG * q
            return feat[:, :, f:f + tr_cols(q) // BS].rearrange("p b f -> p f b")

        def gram_part(ps, s):
            return ps[NP * s:NP * s + NN, 0:GG * NN * SG].rearrange(
                "p (g s m) -> p m g s", g=GG, s=SG)[:, :, :, s]

        def gram_dst(half, blk, q, s):
            b0 = BS * (blk % 2) + GG * SG * q
            v = gram[NP * half:NP * half + NN, :, b0:b0 + GG * SG]
            return v.rearrange("p m (g s) -> p m g s", s=SG)[:, :, :, s]

        N_SMALL = 3
        N_W01 = KX + O0

        block = ctx.enter_context(nc.Block())

        @block.sync
        def _(sp):
            def load_indices(part, k0, k1):
                for j in range(2):
                    sp.dma_start(raw_idx[BS * j:BS * j + BS, k0:k1, :],
                                 sparse[BS * k0:BS * k1, :].rearrange("(k s) t -> s k t", s=BS)
                                 ).then_inc(s_idx[part], 16)

            def stage_free(n):
                if n >= 2:
                    sp.wait_ge(v_split, n - 1)

            def load_w01(n):
                pass

            load_indices(0, 0, 4)
            sp.dma_start(dense_rows[:, :, :], dense.rearrange("(c p) k -> p c k", p=P)).then_inc(s_dense, 16)
            for v, c, n in vectors:
                sp.dma_start(vec_rows[c:c + n, :], v.rearrange("(j p) -> j p", p=P)).then_inc(s_vec, 16)
            sp.dma_start(vec_rows[c_w4:c_w4 + O3, :], tw4.rearrange("(j p) a -> j (p a)", p=P)).then_inc(s_vec, 16)
            sp.dma_start(stage[0:ND, 0, 0:H0], bw0).then_inc(s_stage[0], 16)
            sp.dma_start(stage[:, 1, :].rearrange("p (k n) -> p k n", k=B0),
                         bw1.rearrange("(k p) n -> p k n", p=P)).then_inc(s_stage[1], 16)
            load_indices(1, 4, BLOCKS)
            sp.dma_start(b4[:, :], tb4.rearrange("(a b) -> a b", a=1).partition_broadcast(P)
                         if False else bass.AP(tb4.tensor, 0, [[0, P], [1, 1]])).then_inc(s_b4, 16)
            stage_free(2)
            sp.dma_start(stage[:, 0, 0:B1 * D].rearrange("p (k n) -> p k n", k=B1),
                         bw2.rearrange("(k p) n -> p k n", p=P)).then_inc(s_stage[0], 16)

            def load_top(n):
                stage_free(n)
                k = n - N_SMALL
                slot, done = stage[:, n % 2, :], s_stage[n % 2]
                if k < KX:
                    k0, k1 = (0, P) if k == 0 else (P * k, min(P * k + P, tw0.shape[0]))
                    sp.dma_start(slot[0:k1 - k0, :], tw0[k0:k1, :]).then_inc(done, 16)
                elif k < N_W01:
                    sp.dma_start(slot, tw1[P * (k - KX):P * (k - KX) + P, :]).then_inc(done, 16)
                elif k == N_W01:
                    sp.dma_start(slot.rearrange("p (k n) -> p k n", k=O2),
                                 tw3.rearrange("(k p) n -> p k n", p=P)).then_inc(done, 16)
                else:
                    j = 2 * (k - N_W01 - 1)
                    sp.dma_start(slot.rearrange("p (k n) -> p k n", k=2),
                                 tw2[P * j:P * j + 2 * P, :].rearrange("(k p) n -> p k n", p=P)).then_inc(done, 16)

            def store_dense_out(c):
                sp.wait_ge(v_ev, BEV * c + BEV)
                sp.dma_start(dense_hi[:, C * c:C * c + C], ringB_hi[:, B1, :].bitcast(F32)).then_inc(s_scratch, 16)
                sp.dma_start(dense_lo[:, C * c:C * c + C], ringB_lo[:, B1, :].bitcast(F32)).then_inc(s_scratch, 16)

            def load_feature0(b, first=False):
                if not first:
                    sp.wait_ge(a_tr, QT * (b - 1) + 1)
                    sp.wait_ge(v_tr, QT * (b - 1) + 1)
                sp.dma_start(feat0[:, 0, :], dense_hi[:, bass.ds(b * BS, BS)]).then_inc(s_feat0, 16)
                sp.dma_start(feat0[:, 1, :], dense_lo[:, bass.ds(b * BS, BS)]).then_inc(s_feat0, 16)

            def move_pairs(t, h):
                sp.wait_ge(a_gr, QG * (4 * t + 2 * h + 2))
                sp.wait_ge(v_gr, QG * (4 * t + 2 * h + 2))
                sp.wait_ge(v_x, t)
                for n, m, k, p0, cnt in runs:
                    sp.dma_start(pair_rows[p0:p0 + cnt, k, HALF * h:HALF * h + HALF],
                                 gram[NP * h + n:NP * h + n + 1, m - 1:m - 1 + cnt, :]).then_inc(s_pairs[h], 16)

            def load_x_dense(t):
                sp.wait_ge(p_l0, O0 * t)
                sp.dma_start(x_hi[:, 0, :].bitcast(F32), dense_hi[:, bass.ds(t * C, C)]).then_inc(s_x0, 16)
                sp.dma_start(x_lo[:, 0, :].bitcast(F32), dense_lo[:, bass.ds(t * C, C)]).then_inc(s_x0, 16)

            load_top(3)
            n = 4
            for i in range(4):
                for j in range(2):
                    store_dense_out(2 * i + j)
                    for _ in range((1, 2)[j]):
                        load_top(n)
                        n += 1
                if i == 0:
                    sp.wait_ge(s_scratch, 32)
                load_feature0(i, i == 0)
                if i == 2:
                    move_pairs(0, 0)
            while n < N_SMALL + N_W01 + 1 + O1 // 2:
                if n == N_SMALL + N_W01 + 1:
                    pass
                load_top(n)
                n += 1
            load_feature0(4)
            move_pairs(0, 1)
            sp.wait_ge(v_split, N_SMALL + N_W01 + 1 + O1 // 2)
            sp.wait_ge(s_scratch, 32 * TILES)
            load_x_dense(0)

            def tile(t, blocks):
                b = 4 * t + 5
                load_feature0(b)
                if blocks > 1:
                    load_feature0(b + 1)
                move_pairs(t + 1, 0)
                load_feature0(b + 2)
                load_x_dense(t + 1)
                if blocks > 3:
                    load_feature0(b + 3)
                move_pairs(t + 1, 1)

            with sp.Fori(0, TILES - 2) as t:
                tile(t, 4)
            tile(TILES - 2, 3)
            sp.wait_ge(v_zt, 1)
            sp.dma_start(out.rearrange("(c p) -> c p", p=P), act_f32[0:B // P, 0, 0:P]).then_inc(s_out, 16)
            sp.wait_ge(s_out, 16)

        @block.gpsimd
        def _(gp):
            gp.iota(table_base[:, :], pattern=[[V, NT]], base=0, channel_multiplier=0).then_inc(g_const, 1)
            gp.memset(ident[:, :], 0.0).then_inc(g_const, 1)
            gp.wait_ge(g_const, 2)
            gp.affine_select(out=ident[:, :], in_=ident[:, :], compare_op=ALU.not_equal, fill=1.0, base=0,
                             pattern=[[-1, P]], channel_multiplier=1).then_inc(g_const, 1)

            def gather(i):
                for u in range(SL):
                    gp.indirect_dma_start(rows[i % 2][:, u, :], None, table_rows,
                                          bass.IndirectOffsetOnAxis(ap=idx_cur[:, i, u:u + 1], axis=0)
                                          ).then_inc(s_rows[i % 2], 16)

            gp.wait_ge(v_idx0, 1)
            for i in range(4):
                if i >= 2:
                    gp.wait_ge(p_tr, QT * (i - 1))
                gather(i)
            with gp.Fori(1, TILES) as t:
                for i in range(4):
                    gp.wait_ge(v_idx, 4 * t + i - 3)
                    gp.wait_ge(p_tr, QT * (4 * t + i - 1))
                    gp.sem_inc(g_block, 1)
                    gather(i)

        @block.scalar
        def _(act):
            def split_hi(n, dst, src):
                act.wait_ge(s_stage[n % 2], 16 * (n // 2 + 1))
                act.activation(dst, src, ACT.Copy).then_inc(a_split, 1)

            def split_top(n):
                k = n - N_SMALL
                if k < N_W01:
                    kk = LAST if k == KX - 1 else P
                    split_hi(n, w01_hi[0:kk, k, :], stage[0:kk, n % 2, :])
                elif k == N_W01:
                    split_hi(n, w3_hi[:, :, :].rearrange("p k n -> p (k n)"), stage[:, n % 2, :])
                else:
                    j = 2 * (k - N_W01 - 1)
                    split_hi(n, w2_hi[:, j:j + 2, :].rearrange("p k n -> p (k n)"), stage[:, n % 2, :])

            def layer_hi(count, tile, col, slot):
                ps, hi, _ = tile
                if not (isinstance(count, int) and count < 2):
                    act.wait_ge(v_ev, count - 1)
                act.activation(act_f32[:, slot, :], ps, ACT.Relu, bias=bias[:, col:col + 1])
                act.activation(hi, ps, ACT.Relu, bias=bias[:, col:col + 1]).then_inc(a_ev, 1)

            def bottom(c):
                for o in range(BEV):
                    done = (o | 1) + 1 if o < B0 + B1 else BEV
                    act.wait_ge(p_bot, BEV * c + done)
                    if o == BEV - 1:
                        act.wait_ge(s_scratch, 32 * c)
                    layer_hi(BEV * c + o, bottom_tile(o), c_bb0 + o, (BEV * c + o) % 2)

            def piece(q, b, half, blk, pairs_done):
                ps = piece_bank(q)
                if q < QT:
                    act.wait_ge(p_tr, QT * b + q + 1)
                    if q == 0:
                        act.wait_ge(s_feat0, 32 * (b + 1))
                        act.activation(feat_hi[:, :, 0], feat0[:, 0, :], ACT.Copy)
                    act.activation(feat_of(feat_hi, q), transposed(ps, q), ACT.Copy).then_inc(a_tr, 1)
                else:
                    if q == QT and pairs_done is not None:
                        act.wait_ge(s_pairs[half], PAIR_DMA * pairs_done)
                    act.wait_ge(p_gr, QG * b + q - QT + 1)
                    act.activation(gram_dst(half, blk, q - QT, 0), gram_part(ps, 0), ACT.Copy)
                    act.activation(gram_dst(half, blk, q - QT, 1), gram_part(ps, 1), ACT.Copy).then_inc(a_gr, 1)

            def split_x(t):
                act.wait_ge(s_pairs[0], PAIR_DMA * (t + 1))
                act.wait_ge(s_pairs[1], PAIR_DMA * (t + 1))
                act.wait_ge(p_l0, O0 * t)
                act.activation(x_hi[:, 1:KX - 1, :].rearrange("p k b -> p (k b)"),
                               pair_rows[:, 0:KX - 2, :].rearrange("p k b -> p (k b)"), ACT.Copy)
                act.activation(x_hi[0:LAST, KX - 1, :], pair_rows[0:LAST, KX - 2, :], ACT.Copy).then_inc(a_x, 1)

            act.wait_ge(v_zero, 1)
            act.wait_ge(s_stage[0], 16)
            act.activation(bw0s[0:ND, :], stage[0:ND, 0, 0:H0], ACT.Copy)
            act.activation(bw0s[32:32 + ND, :], stage[0:ND, 0, 0:H0], ACT.Copy).then_inc(a_split, 1)
            split_hi(1, bw1_hi[:, :, :].rearrange("p k n -> p (k n)"), stage[:, 1, 0:B0 * H1])
            for j in range(4):
                act.wait_ge(p_pre, 2 + j)
                act.activation(dense_T[0:ND, 512 * j:512 * j + 512], bank[j][0:ND, :], ACT.Copy)
                act.activation(dense_T[64:64 + ND, 512 * j:512 * j + 512], bank[j][0:ND, :], ACT.Copy
                               ).then_inc(a_pre, 1)
            split_hi(2, bw2_hi[:, :, :].rearrange("p k n -> p (k n)"), stage[:, 0, 0:B1 * D])
            act.wait_ge(v_bias, 1)
            n = N_SMALL
            for i in range(4):
                for j in range(2):
                    bottom(2 * i + j)
                    for _ in range((1, 2)[j]):
                        split_top(n)
                        n += 1
                for q in range(QB):
                    piece(q, i, i // 2, i, None)
            act.wait_ge(p_bot, BEV * TILES)
            while n < N_SMALL + N_W01 + 1 + O1 // 2:
                split_top(n)
                n += 1
            for q in range(QB):
                piece(q, 4, 0, 0, 1)
            act.wait_ge(v_split, N_SMALL + N_W01 + 1 + O1 // 2)
            split_x(0)

            def tile(t, blocks):
                def layer(e, tile, col):
                    layer_hi(EV * t + EV0 + e, tile, col, e % 2)

                def h0(k):
                    act.wait_ge(p_l0, O0 * t + k + 1)
                    if k >= RA:
                        act.wait_ge(p_k1, O0 * t + k - RA + 1)
                    layer(k, h0_tile(k), c_t0 + k)

                def h1(k):
                    act.wait_ge(p_l1, O1 * t + (k | 1) + 1)
                    if k >= RB:
                        act.wait_ge(p_k2, O1 * t + k - RB + 1)
                    layer(O0 + k, h1_tile(k), c_t1 + k)

                def pc(p):
                    i = p // QB
                    if i < blocks:
                        half, done = ((0, None), (1, t + 1), (1, None), (0, t + 2))[i]
                        piece(p % QB, 4 * t + 5 + i, half, i + 1, done)

                h0(0)
                h0(1)
                for k in range(O0):
                    if k + 2 < O0:
                        h0(k + 2)
                    for j in range(3):
                        pc(3 * k + j)
                h1(0)
                h1(1)
                for k in range(O1):
                    if k + 2 < O1:
                        h1(k + 2)
                    if k < O1 - 1:
                        pc(3 * O0 + k)
                for k in range(O2):
                    act.wait_ge(p_l2, O2 * t + (k | 1) + 1)
                    layer(O0 + O1 + k, h2_tile(k), c_t2 + k)
                pc(3 * O0 + O1 - 1)
                for k in range(O3):
                    act.wait_ge(p_l3, O3 * t + O3)
                    layer(O0 + O1 + O2 + k, h3_tile(k), c_t3 + k)
                if blocks:
                    split_x(t + 1)

            with act.Fori(0, TILES - 2) as t:
                tile(t, 4)
            tile(TILES - 2, 3)
            tile(TILES - 1, 0)

        @block.vector
        def _(dve):
            dve.memset(dense_T[:, :].bitcast(F32), 0.0)
            dve.memset(bw0s[:, :].bitcast(F32), 0.0).then_inc(v_zero, 1)
            dve.memset(feat_hi[:, :, NF:NP].bitcast(F32), 0.0)
            dve.memset(feat_lo[:, :, NF:NP].bitcast(F32), 0.0).then_inc(v_zero, 1)
            dve.memset(idx_all[:, BLOCKS, :], 0)
            dve.memset(z[:, :], 0.0).then_inc(v_z, 1)

            def make_indices(part, k0, k1, step):
                dve.wait_ge(s_idx[part], 32)
                dve.tensor_scalar(wrap[:, k0:k1, :], raw_idx[:, k0:k1, :], 0.0, float(V), ALU.is_lt, ALU.mult
                                  ).then_inc(v_i, 1)
                dve.wait_ge(v_i, step + 1)
                dve.tensor_tensor(wrapped[:, k0:k1, :], raw_idx[:, k0:k1, :], wrap[:, k0:k1, :], ALU.add
                                  ).then_inc(v_i, 1)
                dve.wait_ge(v_i, step + 2)
                dve.tensor_scalar(clamped[:, k0:k1, :], wrapped[:, k0:k1, :], 0.0, float(V - 1), ALU.max, ALU.min
                                  ).then_inc(v_i, 1)
                dve.wait_ge(v_i, step + 3)
                for j in range(2):
                    h = slice(BS * j, BS * j + BS)
                    src = clamped[h, k0:k1, :].rearrange("p k (u j) -> p k u j", j=2)[:, :, :, j]
                    base = table_base[h, :].rearrange("p (u j) -> p u j", j=2)[:, :, j].rearrange(
                        "p (a u) -> p a u", a=1).to_broadcast([BS, k1 - k0, SL])
                    last = dve.tensor_tensor(idx_all[h, k0:k1, :], src, base, ALU.add)
                last.then_inc(v_i, 1)
                dve.wait_ge(v_i, step + 4)

            dve.wait_ge(g_const, 1)
            make_indices(0, 0, 4, 0)
            dve.tensor_copy(idx_cur[:, :, :], idx_all[:, 0:4, :]).then_inc(v_idx0, 1)

            def split_lo(n, dst, src, hi):
                dve.wait_ge(a_split, n + 1)
                dve.tensor_tensor(dst, src, hi.bitcast(F32), ALU.subtract).then_inc(v_split, 1)

            def flat(ap):
                return ap.rearrange("p k n -> p (k n)")

            def split_top(n):
                k = n - N_SMALL
                if k < N_W01:
                    kk = LAST if k == KX - 1 else P
                    split_lo(n, w01_lo[0:kk, k, :], stage[0:kk, n % 2, :], w01_hi[0:kk, k, :])
                elif k == N_W01:
                    split_lo(n, flat(w3_lo[:, :, :]), stage[:, n % 2, :], flat(w3_hi[:, :, :]))
                else:
                    j = 2 * (k - N_W01 - 1)
                    split_lo(n, flat(w2_lo[:, j:j + 2, :]), stage[:, n % 2, :], flat(w2_hi[:, j:j + 2, :]))

            split_lo(0, bw0s[64:64 + ND, :], stage[0:ND, 0, 0:H0], bw0s[0:ND, :])
            split_lo(1, flat(bw1_lo[:, :, :]), stage[:, 1, 0:B0 * H1], flat(bw1_hi[:, :, :]))
            for j in range(4):
                dve.wait_ge(a_pre, j + 1)
                dve.tensor_tensor(dense_T[32:32 + ND, 512 * j:512 * j + 512], bank[j][0:ND, :],
                                  dense_T[0:ND, 512 * j:512 * j + 512].bitcast(F32), ALU.subtract).then_inc(v_pre, 1)
            dve.wait_ge(p_pre, 1)
            dve.tensor_copy(bias[:, 0:N_VEC], bank[4][:, 0:N_VEC]).then_inc(v_bias, 1)
            dve.wait_ge(v_bias, 1)
            dve.tensor_copy(w4[:, :, 0], bias[:, c_w4:c_w4 + O3]).then_inc(v_w4, 1)
            dve.wait_ge(v_w4, 1)
            dve.tensor_tensor(w4[:, :, 1], bias[:, c_w4:c_w4 + O3], w4[:, :, 0].bitcast(F32), ALU.subtract
                              ).then_inc(v_w4, 1)
            split_lo(2, flat(bw2_lo[:, :, :]), stage[:, 0, 0:B1 * D], flat(bw2_hi[:, :, :]))
            make_indices(1, 4, BLOCKS, 4)

            def layer_lo(count, tile, slot):
                _, hi, lo = tile
                dve.wait_ge(a_ev, count + 1)
                dve.tensor_tensor(lo, act_f32[:, slot, :], hi.bitcast(F32), ALU.subtract).then_inc(v_ev, 1)

            def bottom(c):
                for o in range(BEV):
                    layer_lo(BEV * c + o, bottom_tile(o), (BEV * c + o) % 2)

            def piece(q, b, half, blk, pairs_done, refresh):
                ps = piece_bank(q)
                if q < QT:
                    dve.wait_ge(a_tr, QT * b + q + 1)
                    if q == 0:
                        dve.wait_ge(s_feat0, 32 * (b + 1))
                        dve.tensor_copy(feat_lo[:, :, 0], feat0[:, 1, :])
                    dve.tensor_tensor(feat_of(feat_lo, q), transposed(ps, q), feat_of(feat_hi, q).bitcast(F32),
                                      ALU.subtract).then_inc(v_tr, 1)
                    if q == QT - 1 and refresh:
                        dve.wait_ge(s_rows[(blk) % 2], 16 * SL * refresh_turn(b, blk))
                        dve.tensor_copy(idx_cur[:, blk % 4, :], idx_all[:, bass.ds(b + 4, 1), :].rearrange(
                            "p a u -> p (a u)")).then_inc(v_idx, 1)
                else:
                    if q == QT and pairs_done is not None:
                        dve.wait_ge(s_pairs[half], PAIR_DMA * pairs_done)
                    dve.wait_ge(p_gr, QG * b + q - QT + 1)
                    dve.tensor_copy(gram_dst(half, blk, q - QT, 2), gram_part(ps, 2))
                    dve.tensor_copy(gram_dst(half, blk, q - QT, 3), gram_part(ps, 3)).then_inc(v_gr, 1)

            def refresh_turn(b, blk):
                return turn[0]

            turn = [0]

            def split_x(t):
                dve.wait_ge(a_x, t + 1)
                dve.tensor_tensor(flat(x_lo[:, 1:KX - 1, :]), flat(pair_rows[:, 0:KX - 2, :]),
                                  flat(x_hi[:, 1:KX - 1, :]).bitcast(F32), ALU.subtract)
                dve.tensor_tensor(x_lo[0:LAST, KX - 1, :], pair_rows[0:LAST, KX - 2, :],
                                  x_hi[0:LAST, KX - 1, :].bitcast(F32), ALU.subtract).then_inc(v_x, 1)

            n = N_SMALL
            for i in range(4):
                for j in range(2):
                    bottom(2 * i + j)
                    for _ in range((1, 2)[j]):
                        split_top(n)
                        n += 1
                for q in range(QB):
                    turn[0] = i // 2 + 1
                    piece(q, i, i // 2, i, None, True)
            while n < N_SMALL + N_W01 + 1 + O1 // 2:
                split_top(n)
                n += 1
            for q in range(QB):
                turn[0] = 3
                piece(q, 4, 0, 0, 1, True)
            split_x(0)

            def tile(t, blocks):
                def layer(e, tile):
                    layer_lo(EV * t + EV0 + e, tile, e % 2)

                def h0(k):
                    layer(k, h0_tile(k))

                def h1(k):
                    layer(O0 + k, h1_tile(k))

                def pc(p):
                    i = p // QB
                    if i < blocks:
                        half, done = ((0, None), (1, t + 1), (1, None), (0, t + 2))[i]
                        turn[0] = 2 * t + (5 + i) // 2 + 1
                        piece(p % QB, 4 * t + 5 + i, half, i + 1, done, blocks == 4)

                h0(0)
                h0(1)
                for k in range(O0):
                    if k + 2 < O0:
                        h0(k + 2)
                    for j in range(3):
                        pc(3 * k + j)
                h1(0)
                h1(1)
                for k in range(O1):
                    if k + 2 < O1:
                        h1(k + 2)
                    if k < O1 - 1:
                        pc(3 * O0 + k)
                for k in range(O2):
                    layer(O0 + O1 + k, h2_tile(k))
                pc(3 * O0 + O1 - 1)
                for k in range(O3):
                    layer(O0 + O1 + O2 + k, h3_tile(k))
                if blocks:
                    split_x(t + 1)
                dve.wait_ge(p_l4, t + 1)
                dve.tensor_reduce(z[:, :], bank[1][:, 0:4].rearrange("p (j w) -> p j w", w=2), AX.X, ALU.add
                                  ).then_inc(v_zs, 1)
                dve.wait_ge(v_zs, t + 1)
                dve.tensor_scalar(z_all[:, bass.ds(2 * t, 2)], z[:, :], b4[:, 0:1], 0.0, ALU.add, ALU.max
                                  ).then_inc(v_z, 1)

            dve.wait_ge(s_b4, 16)
            with dve.Fori(0, TILES - 2) as t:
                tile(t, 4)
            tile(TILES - 2, 3)
            tile(TILES - 1, 0)
            dve.wait_ge(p_z, 1)
            dve.tensor_copy(act_f32[0:B // P, 0, 0:P], bank[2][0:B // P, 0:P]).then_inc(v_zt, 1)

        @block.tensor
        def _(pe):
            def mm3(ps, w_hi, w_lo, r_hi, r_lo, first, last, **kw):
                pe.matmul(ps, w_hi, r_hi, start=first, stop=False, skip_group_check=True)
                pe.matmul(ps, w_hi, r_lo, start=False, stop=False, skip_group_check=True)
                return pe.matmul(ps, w_lo, r_hi, start=False, stop=last, skip_group_check=True)

            def piece(q, b, par, turn):
                ps = piece_bank(q)
                if q < QT:
                    if q == 0:
                        pe.wait_ge(s_rows[par], 16 * SL * turn)
                    for u in range(TG * q, min(SL, TG * q + TG)):
                        last = pe.transpose(ps[:, (u % TG) * P:(u % TG) * P + P], rows[par][:, u, :], ident[:, :])
                    last.then_inc(p_tr, 1)
                else:
                    if q == QT:
                        pe.wait_ge(v_tr, QT * b + QT)
                    for gi in range(GG):
                        g = GG * (q - QT) + gi
                        o = ps[:, gi * NN * SG:(gi + 1) * NN * SG]
                        pe.matmul(o, lhs_of(feat_hi, g), rhs_of(feat_hi, g), start=True, stop=False,
                                  skip_group_check=True)
                        pe.matmul(o, lhs_of(feat_hi, g), rhs_of(feat_lo, g), start=False, stop=False,
                                  skip_group_check=True)
                        last = pe.matmul(o, lhs_of(feat_lo, g), rhs_of(feat_hi, g), start=False, stop=True,
                                         skip_group_check=True)
                    last.then_inc(p_gr, 1)

            def bank_free(q, b):
                q, b = (q - 2, b) if q >= 2 else (q + QB - 2, b - 1)
                if isinstance(b, int) and b < 0:
                    return
                if q < QT:
                    pe.wait_ge(v_tr, QT * b + q + 1)
                else:
                    pe.wait_ge(a_gr, QG * b + q - QT + 1)
                    pe.wait_ge(v_gr, QG * b + q - QT + 1)

            pe.wait_ge(g_const, 3)
            pe.wait_ge(s_vec, 16 * (len(vectors) + 1))
            pe.transpose(bank[4][:, 0:N_VEC], vec_rows[0:N_VEC, :], ident[0:N_VEC, 0:N_VEC]).then_inc(p_pre, 1)
            pe.wait_ge(s_dense, 16)
            for j in range(4):
                for c in range(4):
                    last = pe.transpose(bank[j][0:ND, P * c:P * c + P], dense_rows[:, 4 * j + c, :], ident[:, :])
                last.then_inc(p_pre, 1)

            def bottom(c):
                if c == 0:
                    pe.wait_ge(v_split, N_SMALL)
                    pe.wait_ge(v_pre, 4)
                for o in range(B0):
                    pe.matmul(bank[o // 2][:, C * (o % 2):C * (o % 2) + C], bw0s[:, P * o:P * o + P],
                              dense_T[:, C * c:C * c + C], start=True, stop=True).then_inc(p_bot, 1)
                for o in range(B1):
                    for k in range(B0):
                        if o == 0:
                            pe.wait_ge(v_ev, BEV * c + k + 1)
                        last = mm3(bank[2][:, C * o:C * o + C], bw1_hi[:, k, P * o:P * o + P],
                                   bw1_lo[:, k, P * o:P * o + P], bot0_hi[:, k, :], bot0_lo[:, k, :],
                                   k == 0, k == B0 - 1)
                    last.then_inc(p_bot, 1)
                for k in range(B1):
                    pe.wait_ge(v_ev, BEV * c + B0 + k + 1)
                    last = mm3(bank[3][:, 0:C], bw2_hi[:, k, :], bw2_lo[:, k, :], ringB_hi[:, k, :],
                               ringB_lo[:, k, :], k == 0, k == B1 - 1)
                last.then_inc(p_bot, 1)

            for i in range(4):
                bottom(2 * i)
                bottom(2 * i + 1)
                for q in range(QB):
                    bank_free(q, i)
                    if i == 0 and q == QT:
                        pe.wait_ge(v_zero, 2)
                    piece(q, i, i % 2, i // 2 + 1)
            for q in range(QB):
                bank_free(q, 4)
                piece(q, 4, 0, 3)
            pe.wait_ge(v_split, N_SMALL + N_W01 + 1 + O1 // 2)
            pe.wait_ge(v_w4, 2)
            pe.wait_ge(v_ev, EV0)

            def tile(t, blocks):
                e = EV * t + EV0

                def pc(p):
                    i, q = divmod(p, QB)
                    if i >= blocks:
                        return
                    b = 4 * t + 5 + i
                    bank_free(q, b)
                    piece(q, b, (5 + i) % 2, 2 * t + (5 + i) // 2 + 1)

                def layer0(o):
                    ps = h0_tile(o)[0]
                    if o >= 2:
                        pe.wait_ge(a_ev, e + o - 1)
                    for k in range(KX):
                        kk = LAST if k == KX - 1 else P
                        last = mm3(ps, w01_hi[0:kk, k, P * o:P * o + P],
                                   w01_lo[0:kk, k, P * o:P * o + P], x_hi[0:kk, k, :], x_lo[0:kk, k, :],
                                   k == 0, k == KX - 1)
                    last.then_inc(p_l0, 1)

                def layer1(k, o0, o1):
                    if o0 == 0:
                        pe.wait_ge(v_ev, e + k + 1)
                        if k == 0:
                            pe.wait_ge(v_z, t + 1)
                    for o in range(o0, o1):
                        _, r_hi, r_lo = h0_tile(k)
                        last = mm3(h1_tile(o)[0],
                                   w01_hi[:, KX + k, P * o:P * o + P], w01_lo[:, KX + k, P * o:P * o + P],
                                   r_hi, r_lo, k == 0 and o % 2 == 0, k == O0 - 1)
                        if k == O0 - 1:
                            last.then_inc(p_l1, 1)
                    if o1 == O1 and k < O0 - 1:
                        last.then_inc(p_k1, 1)
                    elif o1 == O1:
                        pe.nop().then_inc(p_k1, 1)

                def layer2(k):
                    pe.wait_ge(v_ev, e + O0 + k + 1)
                    _, r_hi, r_lo = h1_tile(k)
                    for o in range(O2):
                        last = mm3(h2_tile(o)[0], w2_hi[:, k, P * o:P * o + P],
                                   w2_lo[:, k, P * o:P * o + P], r_hi, r_lo,
                                   k == 0 and o % 2 == 0, k == O1 - 1)
                        if k == O1 - 1:
                            last.then_inc(p_l2, 1)
                    if k < O1 - 1:
                        last.then_inc(p_k2, 1)
                    else:
                        pe.nop().then_inc(p_k2, 1)

                pe.wait_ge(v_x, t + 1)
                pe.wait_ge(s_x0, 32 * (t + 1))
                layer0(0)
                layer0(1)
                for k in range(O0):
                    if k + 2 < O0:
                        layer0(k + 2)
                    pc(3 * k)
                    layer1(k, 0, O1 // 2)
                    pc(3 * k + 1)
                    layer1(k, O1 // 2, O1)
                    pc(3 * k + 2)
                for k in range(O1):
                    layer2(k)
                    pc(3 * O0 + k)
                for k in range(O2):
                    pe.wait_ge(v_ev, e + O0 + O1 + k + 1)
                    _, r_hi, r_lo = h2_tile(k)
                    for o in range(O3):
                        last = mm3(h3_tile(o)[0], w3_hi[:, k, P * o:P * o + P],
                                   w3_lo[:, k, P * o:P * o + P], r_hi, r_lo,
                                   k == 0 and o == 0, k == O2 - 1)
                        if k == O2 - 1:
                            last.then_inc(p_l3, 1)
                pe.wait_ge(v_ev, e + EV)
                for j in range(2):
                    for k in range(O3):
                        for s, h in enumerate((ringB_hi, ringB_lo)):
                            last = pe.matmul(bank[1][:, 2 * j:2 * j + 2], h[:, k, P * j:P * j + P], w4[:, k, :],
                                             start=(k == 0 and s == 0), stop=(k == O3 - 1 and s == 1),
                                             skip_group_check=True)
                last.then_inc(p_l4, 1)

            with pe.Fori(0, TILES - 2) as t:
                tile(t, 4)
            tile(TILES - 2, 3)
            tile(TILES - 1, 0)
            pe.wait_ge(v_z, TILES + 1)
            pe.transpose(bank[2][0:B // P, 0:P], z_all[:, :], ident[:, :]).then_inc(p_z, 1)


_NAMES = ["r_dense", "r_sparse", "L0_rec_emb_tables", "L0_rec_bw0", "L0_rec_bb0", "L0_rec_bw1", "L0_rec_bb1",
          "L0_rec_bw2", "L0_rec_bb2", "L0_rec_tw0", "L0_rec_tb0", "L0_rec_tw1", "L0_rec_tb1", "L0_rec_tw2",
          "L0_rec_tb2", "L0_rec_tw3", "L0_rec_tb3", "L0_rec_tw4", "L0_rec_tb4"]


def kernel(**inputs):
    import numpy as np
    import concourse.bacc as bacc
    from concourse.bass_utils import run_bass_kernel_spmd

    nc = bacc.Bacc("TRN2", target_bir_lowering=False, num_devices=1)
    arrays, args = {}, []
    for name in _NAMES:
        a = np.ascontiguousarray(inputs[name])
        arrays[name + "_in"] = a
        args.append(nc.dram_tensor(name + "_in", a.shape, mybir.dt.from_np(a.dtype), kind="ExternalInput").ap())
    out = nc.dram_tensor("scores_out", (inputs["r_dense"].shape[0],), F32, kind="ExternalOutput").ap()
    dlrm(nc, *args, out)
    result = run_bass_kernel_spmd(nc, [arrays], core_ids=[0])
    return result.results[0]["scores_out"]
```

```python
from contextlib import ExitStack

import concourse.bass as bass
from concourse import mybir
from concourse.alu_op_type import AluOpType as ALU

F32 = mybir.dt.float32
F32R = mybir.dt.float32r
I32 = mybir.dt.int32
ACT = mybir.ActivationFunctionType
AX = mybir.AxisListType

P = 128


def dlrm(nc, dense, sparse, emb, bw0, bb0, bw1, bb1, bw2, bb2,
         tw0, tb0, tw1, tb1, tw2, tb2, tw3, tb3, tw4, tb4, out):
    B, ND = dense.shape
    NT, V, D = emb.shape
    NF = NT + 1
    H0, H1 = bw0.shape[1], bw1.shape[1]
    M0, M1, M2, M3 = tw0.shape[1], tw1.shape[1], tw2.shape[1], tw3.shape[1]
    PAIRS = NF * (NF - 1) // 2
    C = 256
    HALF = C // 2
    BS = C // 4
    TILES = B // C
    BLOCKS = B // BS
    SL = NT // 2
    TG = 4
    QT = -(-SL // TG)
    SG = 4
    NN = NF - 1
    NP = 32
    GG = 4
    QG = BS // SG // GG
    QB = QT + QG
    KX = 1 + -(-PAIRS // P)
    O0, O1, O2, O3 = M0 // P, M1 // P, M2 // P, M3 // P
    B0, B1 = H0 // P, H1 // P
    EV = O0 + O1 + O2 + O3
    BEV = B0 + B1 + 1
    RA, RB = 4, 3
    assert (D, NT, C, BS, QT, QG, O0, O1, O2, O3, B0, B1, KX) == (P, 26, 256, 64, 4, 4, 8, 8, 4, 2, 4, 2, 4)

    Q, R = NF // 3, NF // 9
    FIT = P // (NF - Q)
    rectangles = [
        [(0, Q, 0, FIT, NF - Q)],
        [(FIT, Q, 0, Q - FIT, NF - Q), (Q, 2 * Q, 0, Q, Q), (1, 2, 1, Q, 1)],
        [(g, g + R, 0, R, Q - R) for g in (0, Q, 2 * Q)] +
        [(g + R, g + 2 * R, 0, R, R) for g in (0, Q, 2 * Q)] + [(0, 1, 1, Q, R - 1)]]
    pair_tiles = [[(n0 + (R if slope else 1) * r, m0 + slope * R * r + col) for n0, m0, slope, nr, ncols in tile
                   for r in range(nr) for col in range(ncols)] for tile in rectangles]
    assert sorted(sum(pair_tiles, [])) == [(n, m) for n in range(NF) for m in range(n + 1, NF)]
    KROWS = [P] + [len(tile) for tile in pair_tiles]
    assert max(KROWS) <= P

    w0_runs = [(0, 0, 0, D)]
    for k, tile in enumerate(pair_tiles, 1):
        for p, (n, m) in enumerate(tile):
            row = D + n * (2 * NF - n - 1) // 2 + m - n - 1
            k_, p0, row0, cnt = w0_runs[-1]
            if k_ == k and row == row0 + cnt:
                w0_runs[-1] = (k, p0, row0, cnt + 1)
            else:
                w0_runs.append((k, p, row, 1))

    gram_dram = nc.dram_tensor("gram_scratch", (2, NN, NN, HALF), F32, kind="Internal").ap()

    table_rows = emb.rearrange("t v d -> (t v) d")

    with ExitStack() as ctx:
        def sb(name, shape, dt):
            return ctx.enter_context(nc.sbuf_tensor(name, shape, dt))

        def sb_lo(name, shape):
            with nc.sbuf_tensor(name + "_raw", shape, F32) as raw:
                pass
            return sb(name, shape, F32R), raw

        def sem(name):
            return ctx.enter_context(nc.semaphore(name))

        w01_hi = sb("w01_hi", [P, KX + O0, M0], F32R)
        w01_lo, w01_raw = sb_lo("w01_lo", [P, KX + O0, M0])
        w3_hi = sb("w3_hi", [P, O2, M3], F32R)
        w3_lo, w3_raw = sb_lo("w3_lo", [P, O2, M3])
        ringA_hi = sb("ringA_hi", [P, RA, C], F32R)
        ringA_lo = sb("ringA_lo", [P, RA, C], F32R)
        ringB_hi = sb("ringB_hi", [P, RB, C], F32R)
        ringB_lo = sb("ringB_lo", [P, RB, C], F32R)
        pair_rows = sb("pair_rows", [P, KX - 1, C], F32)
        act_f32 = sb("act_f32", [P, 2, C], F32)
        dense_out = sb("dense_out", [P, B], F32)
        feat = sb("feat", [P, BS, NP], F32)
        rows = [sb(f"rows{i}", [P, SL, D], F32) for i in range(2)]
        gram = sb("gram", [P, NN, HALF], F32)
        idx_all = sb("idx_all", [P, BLOCKS + 1, SL], I32)
        idx_cur = sb("idx_cur", [P, 4, SL], I32)
        ident = sb("ident", [P, P], F32)
        bias = sb("bias", [P, 32], F32)
        w4 = sb("w4", [P, O3, 2], F32R)
        b4 = sb("b4", [P, 1], F32)
        z = sb("z", [P, 2], F32)
        z_all = sb("z_all", [P, B // P], F32)

        with nc.sbuf_tensor("bot0_odd", [P, 2, B0, C], F32R) as bot0_odd:
            pass
        x_hi = sb("x_hi", [P, KX, C], F32R)
        x_lo = sb("x_lo", [P, KX, C], F32R)
        with ExitStack() as early:
            dense_T = early.enter_context(nc.sbuf_tensor("dense_T", [96, B], F32R))
            bw0s = early.enter_context(nc.sbuf_tensor("bw0s", [96, H0], F32R))
            bw1_hi = early.enter_context(nc.sbuf_tensor("bw1_hi", [P, B0, H1], F32R))
            with nc.sbuf_tensor("bw1_raw", [P, B0, H1], F32) as bw1_raw:
                pass
            bw1_lo = early.enter_context(nc.sbuf_tensor("bw1_lo", [P, B0, H1], F32R))
            bw2_hi = early.enter_context(nc.sbuf_tensor("bw2_hi", [P, B1, D], F32R))
            with nc.sbuf_tensor("bw2_raw", [P, B1, D], F32) as bw2_raw:
                pass
            bw2_lo = early.enter_context(nc.sbuf_tensor("bw2_lo", [P, B1, D], F32R))
            dense_rows = early.enter_context(nc.sbuf_tensor("dense_rows", [P, B // P, ND], F32))
            table_base = early.enter_context(nc.sbuf_tensor("table_base", [P, NT], I32))
            bw0_raw = early.enter_context(nc.sbuf_tensor("bw0_raw", [32, H0], F32))
            bot0_even = early.enter_context(nc.sbuf_tensor("bot0_even", [P, 2, B0, C], F32R))
            vec_rows = early.enter_context(nc.sbuf_tensor("vec_rows", [32, P], F32))
        w2_hi = sb("w2_hi", [P, O1, M2], F32R)
        w2_lo, w2_raw = sb_lo("w2_lo", [P, O1, M2])

        WI = BLOCKS * NT
        gram_flat = gram[:, :, :].rearrange("p m b -> p (m b)")
        raw_idx = gram_flat[:, 0:WI].bitcast(I32).rearrange("p (k t) -> p k t", t=NT)
        wrap = gram_flat[:, WI:2 * WI].rearrange("p (k t) -> p k t", t=NT)
        wrapped = gram_flat[:, 2 * WI:3 * WI].rearrange("p (k t) -> p k t", t=NT)
        clamped = gram_flat[:, 3 * WI:4 * WI].rearrange("p (k t) -> p k t", t=NT)

        bank = [ctx.enter_context(nc.psum_tensor(f"bank{i}", [P, 512], F32)) for i in range(8)]

        s_idx = [sem("idx_first"), sem("idx_rest")]
        s_vec = sem("vectors_loaded")
        s_b4 = sem("b4_loaded")
        s_dense = sem("dense_loaded")
        s_bw = [sem(f"bw{i}_loaded") for i in range(3)]
        s_tw0 = [sem(f"tw0_ktile{i}_loaded") for i in range(KX)]
        s_tw1 = [sem(f"tw1_part{i}_loaded") for i in range(4)]
        s_tw3 = sem("tw3_loaded")
        s_tw2 = [sem(f"tw2_part{i}_loaded") for i in range(2)]
        s_rows = [sem("rows0_gathered"), sem("rows1_gathered")]
        s_gram = [sem("gram_half0_stored"), sem("gram_half1_stored")]
        s_pairs = [[sem(f"pairs{k}_half{h}_moved") for h in range(2)] for k in range(1, KX)]
        s_out = sem("out_stored")
        g_const = sem("constants_made")
        g_block = sem("gather_begun")
        p_pre = sem("pe_prologue_transposes")
        p_b0, p_b1, p_b2 = sem("pe_bottom0"), sem("pe_bottom1"), sem("pe_bottom2")
        p_tr = sem("pe_transposed")
        p_gr = sem("pe_gram")
        p_l0, p_k1, p_l1, p_k2, p_l2, p_l3, p_l4 = (sem("pe_layer0"), sem("pe_layer1_step"), sem("pe_layer1"),
                                                   sem("pe_layer2_step"), sem("pe_layer2"), sem("pe_layer3"),
                                                   sem("pe_layer4"))
        p_z = sem("pe_out_transposed")
        a_split, v_split = sem("act_weights_hi"), sem("vec_weights_lo")
        a_pre, v_pre = sem("act_dense_hi"), sem("vec_dense_lo")
        v_tr = sem("vec_features")
        v_dense = sem("vec_dense_out")
        a_gr, v_gr = sem("act_gram"), sem("vec_gram")
        a_ev, v_ev = sem("act_layer_hi"), sem("vec_layer_lo")
        a_x, v_x = sem("act_x_hi"), [sem(f"vec_x{k}_lo") for k in range(KX)]
        v_zero = sem("vec_zeroed")
        v_i = sem("vec_index_steps")
        v_idx0 = sem("vec_first_indices")
        v_idx = sem("vec_indices_refreshed")
        v_bias = sem("vec_bias")
        v_w4 = sem("vec_w4")
        v_zs, v_z, v_zt = sem("vec_z_sum"), sem("vec_z"), sem("vec_z_transposed")

        c_bb0, c_bb1, c_bb2 = 0, B0, B0 + B1
        c_t0 = c_bb2 + 1
        c_t1, c_t2, c_t3 = c_t0 + O0, c_t0 + O0 + O1, c_t0 + O0 + O1 + O2
        c_w4 = c_t3 + O3
        vectors = [(bb0, c_bb0, B0), (bb1, c_bb1, B1), (bb2, c_bb2, 1), (tb0, c_t0, O0), (tb1, c_t1, O1),
                   (tb2, c_t2, O2), (tb3, c_t3, O3)]
        N_VEC = c_w4 + O3

        def rhs_of(g):
            return feat[:, SG * g:SG * g + SG, 1:NF]

        def lhs_of(g):
            return feat[:, SG * g:SG * g + SG, :].rearrange("p s n -> p (s n)")[:, 0:NP * (SG - 1) + NN]

        def piece_bank(q):
            return bank[6 + q % 2]

        def half_bank(first, k):
            return bank[first + k // 2][:, C * (k % 2):C * (k % 2) + C]

        def b0_tile(c, k):
            pair = (bot0_even, bot0_odd)[c % 2]
            return half_bank(4 * (c % 2), k), pair[:, 0, k, :], pair[:, 1, k, :]

        def b1_tile(k):
            return half_bank(2, k), ringB_hi[:, k, :], ringB_lo[:, k, :]

        def e_b0(c, k):
            return k + (B0 + (B0 + B1) * (c - 1) if c else 0)

        def e_b1(c, k):
            return k + min(B0 + (B0 + B1) * c + B0, (B0 + B1) * TILES - B1)

        def h0_tile(k):
            return bank[(2, 3)[k] if k < 2 else 4 + k % 2][:, 0:C], ringA_hi[:, k % RA, :], ringA_lo[:, k % RA, :]

        def h1_tile(k):
            return half_bank(0, k), ringB_hi[:, k % RB, :], ringB_lo[:, k % RB, :]

        def h2_tile(k):
            hi, lo, slot = (ringA_hi, ringA_lo, 2 + k) if k < 2 else (ringB_hi, ringB_lo, k - 2)
            return half_bank(4, k), hi[:, slot, :], lo[:, slot, :]

        def h3_tile(k):
            slot = (2, 0)[k]
            return half_bank(0, k), ringB_hi[:, slot, :], ringB_lo[:, slot, :]

        def e_h0(k, first):
            return k + O3 if k or first else 0

        def e_h3(k, last):
            return k if last else k + 1

        E_H1, E_H2 = O3 + O0, O3 + O0 + O1

        def pieces_l1(k, part):
            return [4 * k + part] if k < 6 else []

        def pieces_l2(k):
            return [3 * QB + k]

        X_STEPS = (0, 3, 4, 5)
        L1_PARTS = ((0, 3), (3, 6), (6, 8))

        EV0 = (B0 + B1) * TILES

        def tr_cols(q):
            return (min(SL, TG * (q + 1)) - TG * q) * P

        def transposed(ps, q):
            return ps[:, 0:tr_cols(q)].rearrange("p (f b) -> p f b", b=BS)

        def feat_of(q):
            f = 1 + 2 * TG * q
            return feat[:, :, f:f + tr_cols(q) // BS].rearrange("p b f -> p f b")

        def gram_part(ps, s):
            return ps[NP * s:NP * s + NN, 0:GG * NN * SG].rearrange(
                "p (g s m) -> p m g s", g=GG, s=SG)[:, :, :, s]

        def gram_dst(half, blk, q, s):
            b0 = BS * (blk % 2) + GG * SG * q
            v = gram[NP * half:NP * half + NN, :, b0:b0 + GG * SG]
            return v.rearrange("p m (g s) -> p m g s", s=SG)[:, :, :, s]

        def flat(ap):
            return ap.rearrange("p k n -> p (k n)")

        splits = []
        for k in range(O0):
            splits.append((s_tw1[k // 2], 16, w01_raw[:, KX + k, :], w01_hi[:, KX + k, :], w01_lo[:, KX + k, :]))
        splits.append((s_tw3, 16, flat(w3_raw[:, :, :]), flat(w3_hi[:, :, :]), flat(w3_lo[:, :, :])))
        for k, kk in enumerate(KROWS):
            splits.append((s_tw0[k], 16 * sum(run[0] == k for run in w0_runs),
                           w01_raw[0:kk, k, :], w01_hi[0:kk, k, :], w01_lo[0:kk, k, :]))
        N_EARLY = len(splits)
        for j in range(0, O1, 2):
            splits.append((s_tw2[j // 4], 16, flat(w2_raw[:, j:j + 2, :]), flat(w2_hi[:, j:j + 2, :]),
                           flat(w2_lo[:, j:j + 2, :])))
        N_SMALL = 3

        steps, s0, p0 = [], 0, 0
        for n_splits, before, after in ((3, 0, 0), (3, 0, 0), (2, 2, 2), (1, 2, 2), (1, 2, 2), (1, 2, 2),
                                        (1, 2, 2), (1, 2, 2)):
            steps.append((range(s0, s0 + n_splits), range(p0, p0 + before), range(p0 + before, p0 + before + after)))
            s0, p0 = s0 + n_splits, p0 + before + after
        assert (len(steps), s0, p0) == (TILES, N_EARLY, 3 * QB)

        block = ctx.enter_context(nc.Block())

        @block.sync
        def _(sp):
            def load_indices(part, k0, k1):
                for j in range(2):
                    sp.dma_start(raw_idx[BS * j:BS * j + BS, k0:k1, :],
                                 sparse[BS * k0:BS * k1, :].rearrange("(k s) t -> s k t", s=BS)
                                 ).then_inc(s_idx[part], 16)

            def load_ktiles(dst, w, k0, k1, done):
                sp.dma_start(dst, w[P * k0:P * k1, :].rearrange("(k p) n -> p k n", p=P)
                             ).then_inc(done, 16)

            load_indices(0, 0, 4)
            sp.dma_start(dense_rows[:, :, :], dense.rearrange("(c p) k -> p c k", p=P)).then_inc(s_dense, 16)
            sp.dma_start(bw0_raw[0:ND, :], bw0).then_inc(s_bw[0], 16)
            load_ktiles(bw1_raw[:, :, :], bw1, 0, B0, s_bw[1])
            for v, c, n in vectors:
                sp.dma_start(vec_rows[c:c + n, :], v.rearrange("(j p) -> j p", p=P)).then_inc(s_vec, 16)
            sp.dma_start(vec_rows[c_w4:c_w4 + O3, :], tw4.rearrange("(j p) a -> j (p a)", p=P)).then_inc(s_vec, 16)
            load_ktiles(bw2_raw[:, :, :], bw2, 0, B1, s_bw[2])
            load_indices(1, 4, BLOCKS)
            for j in range(4):
                load_ktiles(w01_raw[:, KX + 2 * j:KX + 2 * j + 2, :], tw1, 2 * j, 2 * j + 2, s_tw1[j])
            load_ktiles(w3_raw[:, :, :], tw3, 0, O2, s_tw3)
            for k, p0, row, cnt in w0_runs:
                sp.dma_start(w01_raw[p0:p0 + cnt, k, :], tw0[row:row + cnt, :]).then_inc(s_tw0[k], 16)
            sp.dma_start(b4[:, :], bass.AP(tb4.tensor, 0, [[0, P], [1, 1]])).then_inc(s_b4, 16)

            def move_pairs(t, h, first=False):
                sp.wait_ge(a_gr, QG * (4 * t + 2 * h + 2))
                sp.wait_ge(v_gr, QG * (4 * t + 2 * h + 2))
                if not first:
                    for k in range(1, KX):
                        sp.wait_ge(v_x[k], t)
                sp.dma_start(gram_dram[h], gram[NP * h:NP * h + NN, :, :]).then_inc(s_gram[h], 16)
                sp.wait_ge(s_gram[h], 16 * t + 16)
                for k, tile in enumerate(rectangles):
                    p0 = 0
                    for n0, m0, slope, nr, ncols in tile:
                        src = bass.AP(gram_dram.tensor, ((h * NN + n0) * NN + m0 - 1) * HALF,
                                      [[(R * (NN + 1) if slope else NN) * HALF, nr], [HALF, ncols], [1, HALF]])
                        p1 = p0 + nr * ncols
                        sp.dma_start(pair_rows[p0:p1, k, HALF * h:HALF * h + HALF], src
                                     ).then_inc(s_pairs[k][h], 16)
                        p0 = p1

            move_pairs(0, 0, True)
            sp.wait_ge(p_b2, TILES)
            for j in range(2):
                load_ktiles(w2_raw[:, 4 * j:4 * j + 4, :], tw2, 4 * j, 4 * j + 4, s_tw2[j])
            move_pairs(0, 1, True)
            with sp.Fori(1, TILES) as t:
                move_pairs(t, 0)
                move_pairs(t, 1)
            sp.wait_ge(v_zt, 1)
            sp.dma_start(out.rearrange("(c p) -> c p", p=P), act_f32[0:B // P, 0, 0:P]).then_inc(s_out, 16)
            sp.wait_ge(s_out, 16)

        @block.gpsimd
        def _(gp):
            gp.iota(table_base[:, :], pattern=[[V, NT]], base=0, channel_multiplier=0).then_inc(g_const, 1)
            gp.memset(ident[:, :], 0.0).then_inc(g_const, 1)
            gp.wait_ge(g_const, 2)
            gp.affine_select(out=ident[:, :], in_=ident[:, :], compare_op=ALU.not_equal, fill=1.0, base=0,
                             pattern=[[-1, P]], channel_multiplier=1).then_inc(g_const, 1)

            def gather(i):
                for u in range(SL):
                    gp.indirect_dma_start(rows[i % 2][:, u, :], None, table_rows,
                                          bass.IndirectOffsetOnAxis(ap=idx_cur[:, i, u:u + 1], axis=0)
                                          ).then_inc(s_rows[i % 2], 16)

            gp.wait_ge(v_idx0, 1)
            for i in range(4):
                if i >= 2:
                    gp.wait_ge(p_tr, QT * (i - 1))
                gather(i)
            with gp.Fori(1, TILES) as t:
                for i in range(4):
                    gp.wait_ge(v_idx, 4 * t + i - 3)
                    gp.wait_ge(p_tr, QT * (4 * t + i - 1))
                    gp.sem_inc(g_block, 1)
                    gather(i)

        @block.scalar
        def _(act):
            def split_hi(loaded, count, raw, hi, _):
                act.wait_ge(loaded, count)
                act.activation(hi, raw, ACT.Copy).then_inc(a_split, 1)

            def layer_hi(count, tile, col, slot):
                ps, hi, _ = tile
                if not (isinstance(count, int) and count < 2):
                    act.wait_ge(v_ev, count - 1)
                act.activation(act_f32[:, slot, :], ps, ACT.Relu, bias=bias[:, col:col + 1])
                act.activation(hi, ps, ACT.Relu, bias=bias[:, col:col + 1]).then_inc(a_ev, 1)

            def bottom0(c):
                for k in range(B0):
                    act.wait_ge(p_b0, B0 * c + (k | 1) + 1)
                    layer_hi(e_b0(c, k), b0_tile(c, k), c_bb0 + k, k % 2)

            def bottom1(c):
                for k in range(B1):
                    act.wait_ge(p_b1, B1 * c + B1)
                    layer_hi(e_b1(c, k), b1_tile(k), c_bb1 + k, k % 2)

            def piece(q, b, half, blk, gram_done):
                if q < QT:
                    return
                if q == QT and gram_done is not None:
                    act.wait_ge(s_gram[half], 16 * gram_done)
                ps = piece_bank(q)
                act.wait_ge(p_gr, QG * b + q - QT + 1)
                act.activation(gram_dst(half, blk, q - QT, 0), gram_part(ps, 0), ACT.Copy)
                act.activation(gram_dst(half, blk, q - QT, 1), gram_part(ps, 1), ACT.Copy).then_inc(a_gr, 1)

            def early_piece(p):
                b = p // QB
                piece(p % QB, b, (0, 0, 1, 1, 0)[b], b, 1 if b == 4 else None)

            def split_x(t, k):
                if k == 0:
                    act.wait_ge(p_l0, O0 * t)
                    src = dense_out[:, bass.ds(t * C, C)]
                else:
                    for h in range(2):
                        act.wait_ge(s_pairs[k - 1][h], 16 * len(rectangles[k - 1]) * (t + 1))
                    src = pair_rows[0:KROWS[k], k - 1, :]
                act.activation(x_hi[0:KROWS[k], k, :], src, ACT.Copy).then_inc(a_x, 1)

            act.wait_ge(v_zero, 1)
            act.wait_ge(s_bw[0], 16)
            act.activation(bw0s[0:ND, :], bw0_raw[0:ND, :], ACT.Copy)
            act.activation(bw0s[32:32 + ND, :], bw0_raw[0:ND, :], ACT.Copy).then_inc(a_split, 1)
            act.wait_ge(v_zero, 2)
            for j in range(4):
                act.wait_ge(p_pre, 1 + j)
                act.activation(dense_T[0:ND, 512 * j:512 * j + 512], bank[j][0:ND, :], ACT.Copy)
                act.activation(dense_T[64:64 + ND, 512 * j:512 * j + 512], bank[j][0:ND, :], ACT.Copy
                               ).then_inc(a_pre, 1)
                if j == 0:
                    split_hi(s_bw[1], 16, flat(bw1_raw[:, :, :]), flat(bw1_hi[:, :, :]), flat(bw1_lo[:, :, :]))
            split_hi(s_bw[2], 16, flat(bw2_raw[:, :, :]), flat(bw2_hi[:, :, :]), flat(bw2_lo[:, :, :]))
            act.wait_ge(v_bias, 1)
            bottom0(0)
            for c, (split_now, before, after) in enumerate(steps):
                if c + 1 < TILES:
                    bottom0(c + 1)
                for p in before:
                    early_piece(p)
                for n in split_now:
                    split_hi(*splits[n])
                bottom1(c)
                for p in after:
                    early_piece(p)
            for p in range(3 * QB, 4 * QB):
                early_piece(p)
            for n in range(N_EARLY, len(splits)):
                split_hi(*splits[n])
            for p in range(4 * QB, 5 * QB):
                early_piece(p)
            act.wait_ge(v_dense, TILES)
            for k in range(KX):
                split_x(0, k)

            def h3(t, last):
                for k in range(O3):
                    act.wait_ge(p_l3, O3 * t + O3)
                    e = e_h3(k, last)
                    layer_hi(EV * (t + 1) + EV0 - O3 + e, h3_tile(k), c_t3 + k, e % 2)

            def tile(t, blocks, first=False):
                def layer(e, tile, col):
                    layer_hi(EV * t + EV0 - O3 + e, tile, col, e % 2)

                def h0(k):
                    act.wait_ge(p_l0, O0 * t + k + 1)
                    if k >= RA:
                        act.wait_ge(p_k1, O0 * t + k - RA + 1)
                    layer(e_h0(k, first), h0_tile(k), c_t0 + k)

                def h1(k):
                    act.wait_ge(p_l1, O1 * t + (k | 1) + 1)
                    if k >= RB:
                        act.wait_ge(p_k2, O1 * t + k - RB + 1)
                    layer(E_H1 + k, h1_tile(k), c_t1 + k)

                def pc(ps):
                    for p in ps:
                        i = p // QB
                        if i < blocks:
                            half, done = ((0, None), (1, t + 1), (1, None), (0, t + 2))[i]
                            piece(p % QB, 4 * t + 5 + i, half, i + 1, done)

                h0(0)
                if not first:
                    h3(t - 1, False)
                h0(1)
                for k in range(O0):
                    if k + 2 < O0:
                        h0(k + 2)
                    for part in range(4):
                        pc(pieces_l1(k, part))
                h1(0)
                h1(1)
                for k in range(O1):
                    if k + 2 < O1:
                        h1(k + 2)
                    if k < O1 - 1:
                        pc(pieces_l2(k))
                    if blocks and k in X_STEPS:
                        split_x(t + 1, X_STEPS.index(k))
                for k in range(O2):
                    act.wait_ge(p_l2, O2 * t + (k | 1) + 1)
                    layer(E_H2 + k, h2_tile(k), c_t2 + k)
                pc(pieces_l2(O1 - 1))

            tile(0, 4, True)
            with act.Fori(1, TILES - 2) as t:
                tile(t, 4)
            tile(TILES - 2, 3)
            tile(TILES - 1, 0)
            h3(TILES - 1, True)

        @block.vector
        def _(dve):
            def make_indices(part, k0, k1, step):
                dve.wait_ge(s_idx[part], 32)
                dve.tensor_scalar(wrap[:, k0:k1, :], raw_idx[:, k0:k1, :], 0.0, float(V), ALU.is_lt, ALU.mult
                                  ).then_inc(v_i, 1)
                dve.wait_ge(v_i, step + 1)
                dve.tensor_tensor(wrapped[:, k0:k1, :], raw_idx[:, k0:k1, :], wrap[:, k0:k1, :], ALU.add
                                  ).then_inc(v_i, 1)
                dve.wait_ge(v_i, step + 2)
                dve.tensor_scalar(clamped[:, k0:k1, :], wrapped[:, k0:k1, :], 0.0, float(V - 1), ALU.max, ALU.min
                                  ).then_inc(v_i, 1)
                dve.wait_ge(v_i, step + 3)
                for j in range(2):
                    h = slice(BS * j, BS * j + BS)
                    src = clamped[h, k0:k1, :].rearrange("p k (u j) -> p k u j", j=2)[:, :, :, j]
                    base = table_base[h, :].rearrange("p (u j) -> p u j", j=2)[:, :, j].rearrange(
                        "p (a u) -> p a u", a=1).to_broadcast([BS, k1 - k0, SL])
                    last = dve.tensor_tensor(idx_all[h, k0:k1, :], src, base, ALU.add)
                last.then_inc(v_i, 1)
                dve.wait_ge(v_i, step + 4)

            dve.wait_ge(g_const, 1)
            make_indices(0, 0, 4, 0)
            dve.tensor_copy(idx_cur[:, :, :], idx_all[:, 0:4, :]).then_inc(v_idx0, 1)

            dve.memset(bw0s[:, :].bitcast(F32), 0.0).then_inc(v_zero, 1)
            dve.memset(dense_T[:, :].bitcast(F32), 0.0).then_inc(v_zero, 1)
            dve.memset(feat[:, :, NF:NP], 0.0).then_inc(v_zero, 1)
            dve.memset(idx_all[:, BLOCKS, :], 0)
            dve.memset(z[:, :], 0.0).then_inc(v_z, 1)

            def split_lo(n, raw, hi, lo):
                dve.wait_ge(a_split, n + 1)
                dve.tensor_tensor(lo, raw, hi.bitcast(F32), ALU.subtract).then_inc(v_split, 1)

            dve.wait_ge(a_split, 1)
            dve.tensor_tensor(bw0s[64:64 + ND, :], bw0_raw[0:ND, :], bw0s[0:ND, :].bitcast(F32), ALU.subtract
                              ).then_inc(v_split, 1)
            for j in range(4):
                dve.wait_ge(a_pre, j + 1)
                dve.tensor_tensor(dense_T[32:32 + ND, 512 * j:512 * j + 512], bank[j][0:ND, :],
                                  dense_T[0:ND, 512 * j:512 * j + 512].bitcast(F32), ALU.subtract).then_inc(v_pre, 1)
                if j == 0:
                    split_lo(1, flat(bw1_raw[:, :, :]), flat(bw1_hi[:, :, :]), flat(bw1_lo[:, :, :]))
            dve.wait_ge(p_pre, 5)
            dve.tensor_copy(bias[:, 0:N_VEC], bank[4][:, 0:N_VEC]).then_inc(v_bias, 1)
            dve.wait_ge(v_bias, 1)
            dve.tensor_copy(w4[:, :, 0], bias[:, c_w4:c_w4 + O3]).then_inc(v_w4, 1)
            dve.wait_ge(v_w4, 1)
            dve.tensor_tensor(w4[:, :, 1], bias[:, c_w4:c_w4 + O3], w4[:, :, 0].bitcast(F32), ALU.subtract
                              ).then_inc(v_w4, 1)
            split_lo(2, flat(bw2_raw[:, :, :]), flat(bw2_hi[:, :, :]), flat(bw2_lo[:, :, :]))
            make_indices(1, 4, BLOCKS, 4)

            def layer_lo(count, tile, slot):
                _, hi, lo = tile
                dve.wait_ge(a_ev, count + 1)
                dve.tensor_tensor(lo, act_f32[:, slot, :], hi.bitcast(F32), ALU.subtract).then_inc(v_ev, 1)

            def bottom0(c):
                for k in range(B0):
                    layer_lo(e_b0(c, k), b0_tile(c, k), k % 2)

            def bottom1(c):
                for k in range(B1):
                    layer_lo(e_b1(c, k), b1_tile(k), k % 2)

            def bottom2(c):
                dve.wait_ge(p_b2, c + 1)
                dve.tensor_scalar(dense_out[:, C * c:C * c + C], bank[3][:, 0:C], bias[:, c_bb2:c_bb2 + 1], 0.0,
                                  ALU.add, ALU.max).then_inc(v_dense, 1)

            def piece(q, b, half, blk, gram_done, turn, refresh):
                ps = piece_bank(q)
                if q < QT:
                    dve.wait_ge(p_tr, QT * b + q + 1)
                    if q == QT - 1:
                        dve.wait_ge(v_dense, b // 4 + 1 if isinstance(b, int) else TILES)
                        dve.tensor_copy(feat[:, :, 0], dense_out[:, bass.ds(b * BS, BS)])
                    dve.tensor_copy(feat_of(q), transposed(ps, q)).then_inc(v_tr, 1)
                    if q == QT - 1 and refresh:
                        dve.wait_ge(s_rows[blk % 2], 16 * SL * turn)
                        dve.tensor_copy(idx_cur[:, blk % 4, :], idx_all[:, bass.ds(b + 4, 1), :].rearrange(
                            "p a u -> p (a u)")).then_inc(v_idx, 1)
                else:
                    if q == QT and gram_done is not None:
                        dve.wait_ge(s_gram[half], 16 * gram_done)
                    dve.wait_ge(p_gr, QG * b + q - QT + 1)
                    dve.tensor_copy(gram_dst(half, blk, q - QT, 2), gram_part(ps, 2))
                    dve.tensor_copy(gram_dst(half, blk, q - QT, 3), gram_part(ps, 3)).then_inc(v_gr, 1)

            def early_piece(p):
                b = p // QB
                piece(p % QB, b, (0, 0, 1, 1, 0)[b], b % 4, 1 if b == 4 else None, b // 2 + 1, True)

            def split_x(t, k):
                dve.wait_ge(a_x, KX * t + k + 1)
                src = pair_rows[0:KROWS[k], k - 1, :] if k else dense_out[:, bass.ds(t * C, C)]
                dve.tensor_tensor(x_lo[0:KROWS[k], k, :], src, x_hi[0:KROWS[k], k, :].bitcast(F32),
                                  ALU.subtract).then_inc(v_x[k], 1)

            bottom0(0)
            for c, (split_now, before, after) in enumerate(steps):
                if c + 1 < TILES:
                    bottom0(c + 1)
                for p in before:
                    early_piece(p)
                for n in split_now:
                    split_lo(N_SMALL + n, *splits[n][2:])
                bottom1(c)
                for p in after:
                    early_piece(p)
                bottom2(c)
            for p in range(3 * QB, 4 * QB):
                early_piece(p)
            for n in range(N_EARLY, len(splits)):
                split_lo(N_SMALL + n, *splits[n][2:])
            for p in range(4 * QB, 5 * QB):
                early_piece(p)
            for k in range(KX):
                split_x(0, k)

            def h3(t, last):
                for k in range(O3):
                    e = e_h3(k, last)
                    layer_lo(EV * (t + 1) + EV0 - O3 + e, h3_tile(k), e % 2)

            def score(t):
                dve.wait_ge(p_l4, t + 1)
                dve.tensor_reduce(z[:, :], bank[1][:, 0:4].rearrange("p (j w) -> p j w", w=2), AX.X, ALU.add
                                  ).then_inc(v_zs, 1)
                dve.wait_ge(v_zs, t + 1)
                dve.tensor_scalar(z_all[:, bass.ds(2 * t, 2)], z[:, :], b4[:, 0:1], 0.0, ALU.add, ALU.max
                                  ).then_inc(v_z, 1)

            def tile(t, blocks, first=False):
                def layer(e, tile):
                    layer_lo(EV * t + EV0 - O3 + e, tile, e % 2)

                def pc(ps):
                    for p in ps:
                        i = p // QB
                        if i < blocks:
                            half, done = ((0, None), (1, t + 1), (1, None), (0, t + 2))[i]
                            piece(p % QB, 4 * t + 5 + i, half, i + 1, done, 2 * t + (5 + i) // 2 + 1, blocks == 4)

                layer(e_h0(0, first), h0_tile(0))
                if not first:
                    h3(t - 1, False)
                layer(e_h0(1, first), h0_tile(1))
                for k in range(O0):
                    if k + 2 < O0:
                        layer(e_h0(k + 2, first), h0_tile(k + 2))
                    for part in range(4):
                        pc(pieces_l1(k, part))
                        if k == 0 and part == 0 and not first:
                            score(t - 1)
                layer(E_H1, h1_tile(0))
                layer(E_H1 + 1, h1_tile(1))
                for k in range(O1):
                    if k + 2 < O1:
                        layer(E_H1 + k + 2, h1_tile(k + 2))
                    if k < O1 - 1:
                        pc(pieces_l2(k))
                    if blocks and k in X_STEPS:
                        split_x(t + 1, X_STEPS.index(k))
                for k in range(O2):
                    layer(E_H2 + k, h2_tile(k))
                pc(pieces_l2(O1 - 1))

            dve.wait_ge(s_b4, 16)
            tile(0, 4, True)
            with dve.Fori(1, TILES - 2) as t:
                tile(t, 4)
            tile(TILES - 2, 3)
            tile(TILES - 1, 0)
            h3(TILES - 1, True)
            score(TILES - 1)
            dve.wait_ge(p_z, 1)
            dve.tensor_copy(act_f32[0:B // P, 0, 0:P], bank[2][0:B // P, 0:P]).then_inc(v_zt, 1)

        @block.tensor
        def _(pe):
            def mm3(ps, w_hi, w_lo, r_hi, r_lo, first, last, **kw):
                pe.matmul(ps, w_hi, r_hi, start=first, stop=False, skip_group_check=True)
                pe.matmul(ps, w_hi, r_lo, start=False, stop=False, skip_group_check=True)
                return pe.matmul(ps, w_lo, r_hi, start=False, stop=last, skip_group_check=True)

            def piece(q, b, par, turn):
                ps = piece_bank(q)
                if q < QT:
                    if q == 0:
                        pe.wait_ge(s_rows[par], 16 * SL * turn)
                    for u in range(TG * q, min(SL, TG * q + TG)):
                        last = pe.transpose(ps[:, (u % TG) * P:(u % TG) * P + P], rows[par][:, u, :], ident[:, :])
                    last.then_inc(p_tr, 1)
                else:
                    if q == QT:
                        pe.wait_ge(v_tr, QT * b + QT)
                    for gi in range(GG):
                        g = GG * (q - QT) + gi
                        o = ps[:, gi * NN * SG:(gi + 1) * NN * SG]
                        last = pe.matmul(o[0:NP * (SG - 1) + NN, :], lhs_of(g), rhs_of(g), start=True, stop=True)
                    last.then_inc(p_gr, 1)

            def bank_free(q, b):
                q, b = (q - 2, b) if q >= 2 else (q + QB - 2, b - 1)
                if isinstance(b, int) and b < 0:
                    return
                if q < QT:
                    pe.wait_ge(v_tr, QT * b + q + 1)
                else:
                    pe.wait_ge(a_gr, QG * b + q - QT + 1)
                    pe.wait_ge(v_gr, QG * b + q - QT + 1)

            pe.wait_ge(g_const, 3)
            pe.wait_ge(s_dense, 16)
            for j in range(4):
                for c in range(4):
                    last = pe.transpose(bank[j][0:ND, P * c:P * c + P], dense_rows[:, 4 * j + c, :], ident[:, :])
                last.then_inc(p_pre, 1)
            pe.wait_ge(s_vec, 16 * (len(vectors) + 1))
            pe.transpose(bank[4][:, 0:N_VEC], vec_rows[0:N_VEC, :], ident[0:N_VEC, 0:N_VEC]).then_inc(p_pre, 1)

            def bottom0(c):
                if c == 1:
                    pe.wait_ge(v_bias, 1)
                if c >= 2:
                    pe.wait_ge(a_ev, e_b0(c - 2, B0 - 1) + 1)
                for k in range(B0):
                    pe.matmul(b0_tile(c, k)[0], bw0s[:, P * k:P * k + P], dense_T[:, C * c:C * c + C],
                              start=True, stop=True).then_inc(p_b0, 1)

            def bottom1(c):
                for o in range(B1):
                    for k in range(B0):
                        if o == 0:
                            pe.wait_ge(v_ev, e_b0(c, k) + 1)
                        _, r_hi, r_lo = b0_tile(c, k)
                        last = mm3(b1_tile(o)[0], bw1_hi[:, k, P * o:P * o + P], bw1_lo[:, k, P * o:P * o + P],
                                   r_hi, r_lo, k == 0, k == B0 - 1)
                    last.then_inc(p_b1, 1)

            def bottom2(c):
                if c > 0:
                    pe.wait_ge(v_dense, c)
                for k in range(B1):
                    pe.wait_ge(v_ev, e_b1(c, k) + 1)
                    last = mm3(bank[3][:, 0:C], bw2_hi[:, k, :], bw2_lo[:, k, :], ringB_hi[:, k, :],
                               ringB_lo[:, k, :], k == 0, k == B1 - 1)
                last.then_inc(p_b2, 1)

            def early_piece(p):
                b, q = divmod(p, QB)
                bank_free(q, b)
                piece(q, b, b % 2, b // 2 + 1)

            pe.wait_ge(v_split, N_SMALL)
            pe.wait_ge(v_pre, 4)
            pe.wait_ge(v_zero, 3)
            bottom0(0)
            for c, (_, before, after) in enumerate(steps):
                if c + 1 < TILES:
                    bottom0(c + 1)
                for p in before:
                    early_piece(p)
                bottom1(c)
                for p in after:
                    early_piece(p)
                bottom2(c)
            for p in range(3 * QB, 5 * QB):
                early_piece(p)
            pe.wait_ge(v_split, N_SMALL + len(splits))
            pe.wait_ge(v_w4, 2)
            pe.wait_ge(v_dense, TILES)

            def tile(t, blocks, first=False):
                e = EV * t + EV0 - O3

                def pc(ps):
                    for p in ps:
                        i, q = divmod(p, QB)
                        if i < blocks:
                            b = 4 * t + 5 + i
                            bank_free(q, b)
                            piece(q, b, (5 + i) % 2, 2 * t + (5 + i) // 2 + 1)

                def layer0(o):
                    ps = h0_tile(o)[0]
                    if o >= 4:
                        pe.wait_ge(a_ev, e + e_h0(o - 2, first) + 1)
                    for k, kk in enumerate(KROWS):
                        if o == 0:
                            pe.wait_ge(v_x[k], t + 1)
                        last = mm3(ps, w01_hi[0:kk, k, P * o:P * o + P],
                                   w01_lo[0:kk, k, P * o:P * o + P], x_hi[0:kk, k, :], x_lo[0:kk, k, :],
                                   k == 0, k == KX - 1)
                    last.then_inc(p_l0, 1)

                def layer1(k, o0, o1):
                    if o0 == 0:
                        pe.wait_ge(v_ev, e + e_h0(k, first) + 1)
                    for o in range(o0, o1):
                        if k == 0 and o == 2:
                            pe.wait_ge(v_z, t + 1)
                        if k == 0 and o == 6:
                            pe.wait_ge(a_ev, e + e_h0(1, first) + 1)
                        _, r_hi, r_lo = h0_tile(k)
                        last = mm3(h1_tile(o)[0],
                                   w01_hi[:, KX + k, P * o:P * o + P], w01_lo[:, KX + k, P * o:P * o + P],
                                   r_hi, r_lo, k == 0 and o % 2 == 0, k == O0 - 1)
                        if k == O0 - 1:
                            last.then_inc(p_l1, 1)
                    if o1 == O1 and k < O0 - 1:
                        last.then_inc(p_k1, 1)
                    elif o1 == O1:
                        pe.nop().then_inc(p_k1, 1)

                def layer2(k):
                    pe.wait_ge(v_ev, e + E_H1 + k + 1)
                    _, r_hi, r_lo = h1_tile(k)
                    for o in range(O2):
                        last = mm3(h2_tile(o)[0], w2_hi[:, k, P * o:P * o + P],
                                   w2_lo[:, k, P * o:P * o + P], r_hi, r_lo,
                                   k == 0 and o % 2 == 0, k == O1 - 1)
                        if k == O1 - 1:
                            last.then_inc(p_l2, 1)
                    if k < O1 - 1:
                        last.then_inc(p_k2, 1)
                    else:
                        pe.nop().then_inc(p_k2, 1)

                layer0(0)
                if not first:
                    layer3(t - 1)
                layer0(1)
                for k in range(O0):
                    if k + 2 < O0 and k > 0:
                        layer0(k + 2)
                    pc(pieces_l1(k, 0))
                    if k == 0:
                        if not first:
                            layer4(t - 1, False)
                        layer0(2)
                    for part, (o0, o1) in enumerate(L1_PARTS):
                        layer1(k, o0, o1)
                        pc(pieces_l1(k, part + 1))
                for k in range(O1):
                    layer2(k)
                    pc(pieces_l2(k))

            def layer3(t):
                for k in range(O2):
                    pe.wait_ge(v_ev, EV * t + EV0 - O3 + E_H2 + k + 1)
                    _, r_hi, r_lo = h2_tile(k)
                    for o in range(O3):
                        last = mm3(h3_tile(o)[0], w3_hi[:, k, P * o:P * o + P],
                                   w3_lo[:, k, P * o:P * o + P], r_hi, r_lo,
                                   k == 0 and o == 0, k == O2 - 1)
                        if k == O2 - 1:
                            last.then_inc(p_l3, 1)

            def layer4(t, last_pass):
                pe.wait_ge(v_ev, EV * (t + 1) + EV0 - O3 + e_h3(O3 - 1, last_pass) + 1)
                for j in range(2):
                    for k in range(O3):
                        for s, h in enumerate(h3_tile(k)[1:]):
                            last = pe.matmul(bank[1][:, 2 * j:2 * j + 2], h[:, P * j:P * j + P], w4[:, k, :],
                                             start=(k == 0 and s == 0), stop=(k == O3 - 1 and s == 1),
                                             skip_group_check=True)
                last.then_inc(p_l4, 1)

            tile(0, 4, True)
            with pe.Fori(1, TILES - 2) as t:
                tile(t, 4)
            tile(TILES - 2, 3)
            tile(TILES - 1, 0)
            layer3(TILES - 1)
            layer4(TILES - 1, True)
            pe.wait_ge(v_z, TILES + 1)
            pe.transpose(bank[2][0:B // P, 0:P], z_all[:, :], ident[:, :]).then_inc(p_z, 1)


_NAMES = ["r_dense", "r_sparse", "L0_rec_emb_tables", "L0_rec_bw0", "L0_rec_bb0", "L0_rec_bw1", "L0_rec_bb1",
          "L0_rec_bw2", "L0_rec_bb2", "L0_rec_tw0", "L0_rec_tb0", "L0_rec_tw1", "L0_rec_tb1", "L0_rec_tw2",
          "L0_rec_tb2", "L0_rec_tw3", "L0_rec_tb3", "L0_rec_tw4", "L0_rec_tb4"]


def kernel(**inputs):
    import numpy as np
    import concourse.bacc as bacc
    from concourse.bass_utils import run_bass_kernel_spmd

    nc = bacc.Bacc("TRN2", target_bir_lowering=False, num_devices=1)
    arrays, args = {}, []
    for name in _NAMES:
        a = np.ascontiguousarray(inputs[name])
        arrays[name + "_in"] = a
        args.append(nc.dram_tensor(name + "_in", a.shape, mybir.dt.from_np(a.dtype), kind="ExternalInput").ap())
    out = nc.dram_tensor("scores_out", (inputs["r_dense"].shape[0],), F32, kind="ExternalOutput").ap()
    dlrm(nc, *args, out)
    result = run_bass_kernel_spmd(nc, [arrays], core_ids=[0])
    return result.results[0]["scores_out"]
```

```python
from contextlib import ExitStack

import concourse.bass as bass
from concourse import mybir
from concourse.alu_op_type import AluOpType as ALU

F32 = mybir.dt.float32
F32R = mybir.dt.float32r
I32 = mybir.dt.int32
ACT = mybir.ActivationFunctionType
AX = mybir.AxisListType

P = 128


def dlrm(nc, dense, sparse, emb, bw0, bb0, bw1, bb1, bw2, bb2,
         tw0, tb0, tw1, tb1, tw2, tb2, tw3, tb3, tw4, tb4, out):
    B, ND = dense.shape
    NT, V, D = emb.shape
    NF = NT + 1
    H0, H1 = bw0.shape[1], bw1.shape[1]
    M0, M1, M2, M3 = tw0.shape[1], tw1.shape[1], tw2.shape[1], tw3.shape[1]
    PAIRS = NF * (NF - 1) // 2
    C = 256
    HALF = C // 2
    BS = C // 4
    TILES = B // C
    BLOCKS = B // BS
    SL = NT // 2
    TG = 4
    QT = -(-SL // TG)
    SG = 4
    NN = NF - 1
    NP = 32
    GG = 4
    QG = BS // SG // GG
    QB = QT + QG
    KX = 1 + -(-PAIRS // P)
    O0, O1, O2, O3 = M0 // P, M1 // P, M2 // P, M3 // P
    B0, B1 = H0 // P, H1 // P
    EV = O0 + O1 + O2 + O3
    RA, RB = 4, 3
    assert (D, NT, C, BS, QT, QG, O0, O1, O2, O3, B0, B1, KX) == (P, 26, 256, 64, 4, 4, 8, 8, 4, 2, 4, 2, 4)

    Q, R = NF // 3, NF // 9
    FIT = P // (NF - Q)
    rectangles = [
        [(0, Q, 0, FIT, NF - Q)],
        [(FIT, Q, 0, Q - FIT, NF - Q), (Q, 2 * Q, 0, Q, Q), (1, 2, 1, Q, 1)],
        [(g, g + R, 0, R, Q - R) for g in (0, Q, 2 * Q)] +
        [(g + R, g + 2 * R, 0, R, R) for g in (0, Q, 2 * Q)] + [(0, 1, 1, Q, R - 1)]]
    pair_tiles = [[(n0 + (R if slope else 1) * r, m0 + slope * R * r + col) for n0, m0, slope, nr, ncols in tile
                   for r in range(nr) for col in range(ncols)] for tile in rectangles]
    assert sorted(sum(pair_tiles, [])) == [(n, m) for n in range(NF) for m in range(n + 1, NF)]
    KROWS = [P] + [len(tile) for tile in pair_tiles]
    assert max(KROWS) <= P

    w0_runs = [(0, 0, 0, D)]
    for k, tile in enumerate(pair_tiles, 1):
        for p, (n, m) in enumerate(tile):
            row = D + n * (2 * NF - n - 1) // 2 + m - n - 1
            k_, p0, row0, cnt = w0_runs[-1]
            if k_ == k and row == row0 + cnt:
                w0_runs[-1] = (k, p0, row0, cnt + 1)
            else:
                w0_runs.append((k, p, row, 1))

    gram_dram = nc.dram_tensor("gram_scratch", (2, NN, NN, HALF), F32, kind="Internal").ap()

    table_rows = emb.rearrange("t v d -> (t v) d")

    with ExitStack() as ctx:
        def sb(name, shape, dt):
            return ctx.enter_context(nc.sbuf_tensor(name, shape, dt))

        def sb_lo(name, shape):
            with nc.sbuf_tensor(name + "_raw", shape, F32) as raw:
                pass
            return sb(name, shape, F32R), raw

        def sem(name):
            return ctx.enter_context(nc.semaphore(name))

        w01_hi = sb("w01_hi", [P, KX + O0, M0], F32R)
        w01_lo, w01_raw = sb_lo("w01_lo", [P, KX + O0, M0])
        w3_hi = sb("w3_hi", [P, O2, M3], F32R)
        w3_lo, w3_raw = sb_lo("w3_lo", [P, O2, M3])
        ringA_hi = sb("ringA_hi", [P, RA, C], F32R)
        ringA_lo = sb("ringA_lo", [P, RA, C], F32R)
        ringB_hi = sb("ringB_hi", [P, RB, C], F32R)
        ringB_lo = sb("ringB_lo", [P, RB, C], F32R)
        pair_rows = sb("pair_rows", [P, KX - 1, C], F32)
        act_f32 = sb("act_f32", [P, 2, C], F32)
        dense_out = sb("dense_out", [P, B], F32)
        feat = sb("feat", [P, BS, NP], F32)
        rows = [sb(f"rows{i}", [P, SL, D], F32) for i in range(2)]
        gram = sb("gram", [P, NN, HALF], F32)
        idx_all = sb("idx_all", [P, BLOCKS + 1, SL], I32)
        idx_cur = sb("idx_cur", [P, 4, SL], I32)
        ident = sb("ident", [P, P], F32)
        bias = sb("bias", [P, 32], F32)
        w4 = sb("w4", [P, O3, 2], F32R)
        b4 = sb("b4", [P, 1], F32)
        z = sb("z", [P, 2], F32)
        z_all = sb("z_all", [P, B // P], F32)

        with nc.sbuf_tensor("bot0_odd", [P, 2, B0, C], F32R) as bot0_odd:
            pass
        x_hi = sb("x_hi", [P, KX, C], F32R)
        x_lo = sb("x_lo", [P, KX, C], F32R)
        with ExitStack() as early:
            dense_T = early.enter_context(nc.sbuf_tensor("dense_T", [96, B], F32R))
            bw0s = early.enter_context(nc.sbuf_tensor("bw0s", [96, H0], F32R))
            bw1_hi = early.enter_context(nc.sbuf_tensor("bw1_hi", [P, B0, H1], F32R))
            with nc.sbuf_tensor("bw1_raw", [P, B0, H1], F32) as bw1_raw:
                pass
            bw1_lo = early.enter_context(nc.sbuf_tensor("bw1_lo", [P, B0, H1], F32R))
            bw2_hi = early.enter_context(nc.sbuf_tensor("bw2_hi", [P, B1, D], F32R))
            with nc.sbuf_tensor("bw2_raw", [P, B1, D], F32) as bw2_raw:
                pass
            bw2_lo = early.enter_context(nc.sbuf_tensor("bw2_lo", [P, B1, D], F32R))
            table_base = early.enter_context(nc.sbuf_tensor("table_base", [P, NT], I32))
            bw0_raw = early.enter_context(nc.sbuf_tensor("bw0_raw", [32, H0], F32))
            bot0_even = early.enter_context(nc.sbuf_tensor("bot0_even", [P, 2, B0, C], F32R))
            vec_rows = early.enter_context(nc.sbuf_tensor("vec_rows", [32, P], F32))
        w2_hi = sb("w2_hi", [P, O1, M2], F32R)
        w2_lo, w2_raw = sb_lo("w2_lo", [P, O1, M2])

        dense_rows = pair_rows[:, 0:2, :].rearrange("p k (c r) -> p (k c) r", r=NP)

        WI = BLOCKS * NT
        gram_flat = gram[:, :, :].rearrange("p m b -> p (m b)")
        raw_idx = gram_flat[:, 0:WI].bitcast(I32).rearrange("p (k t) -> p k t", t=NT)
        wrap = gram_flat[:, WI:2 * WI].rearrange("p (k t) -> p k t", t=NT)
        wrapped = gram_flat[:, 2 * WI:3 * WI].rearrange("p (k t) -> p k t", t=NT)
        clamped = gram_flat[:, 3 * WI:4 * WI].rearrange("p (k t) -> p k t", t=NT)

        bank = [ctx.enter_context(nc.psum_tensor(f"bank{i}", [P, 512], F32)) for i in range(8)]

        s_idx = [sem("idx_first"), sem("idx_rest")]
        s_vec = sem("vectors_loaded")
        s_b4 = sem("b4_loaded")
        s_dense = sem("dense_loaded")
        s_bw = [sem(f"bw{i}_loaded") for i in range(3)]
        s_tw0 = [sem(f"tw0_ktile{i}_loaded") for i in range(KX)]
        s_tw1 = [sem(f"tw1_part{i}_loaded") for i in range(4)]
        s_tw3 = sem("tw3_loaded")
        s_tw2 = [sem(f"tw2_part{i}_loaded") for i in range(2)]
        s_rows = [sem("rows0_gathered"), sem("rows1_gathered")]
        s_gram = [sem("gram_half0_stored"), sem("gram_half1_stored")]
        s_pairs = [[sem(f"pairs{k}_half{h}_moved") for h in range(2)] for k in range(1, KX)]
        s_out = sem("out_stored")
        g_const = sem("constants_made")
        g_block = sem("gather_begun")
        p_pre = sem("pe_prologue_transposes")
        p_b0, p_b1, p_b2 = sem("pe_bottom0"), sem("pe_bottom1"), sem("pe_bottom2")
        p_tr = sem("pe_transposed")
        p_gr = sem("pe_gram")
        p_l0, p_k1, p_l1, p_k2, p_l2, p_l3, p_l4 = (sem("pe_layer0"), sem("pe_layer1_step"), sem("pe_layer1"),
                                                   sem("pe_layer2_step"), sem("pe_layer2"), sem("pe_layer3"),
                                                   sem("pe_layer4"))
        p_z = sem("pe_out_transposed")
        a_split, v_split = sem("act_weights_hi"), sem("vec_weights_lo")
        a_pre, v_pre = sem("act_dense_hi"), sem("vec_dense_lo")
        a_tr, v_tr = sem("act_features"), sem("vec_features")
        v_dense = sem("vec_dense_out")
        a_gr, v_gr = sem("act_gram"), sem("vec_gram")
        a_b0, v_b0 = sem("act_bottom0_hi"), sem("vec_bottom0_lo")
        a_ev, v_ev = sem("act_layer_hi"), sem("vec_layer_lo")
        a_x, v_x = sem("act_x_hi"), [sem(f"vec_x{k}_lo") for k in range(KX)]
        v_one = sem("vec_ones")
        v_zero = sem("vec_zeroed")
        v_i = sem("vec_index_steps")
        v_idx0 = sem("vec_first_indices")
        v_idx = sem("vec_indices_refreshed")
        v_bias = sem("vec_bias")
        v_w4 = sem("vec_w4")
        v_zs, v_z, v_zt = sem("vec_z_sum"), sem("vec_z"), sem("vec_z_transposed")

        c_bb1, c_bb2 = 0, B1
        c_t0 = c_bb2 + 1
        c_t1, c_t2, c_t3 = c_t0 + O0, c_t0 + O0 + O1, c_t0 + O0 + O1 + O2
        c_w4 = c_t3 + O3
        vectors = [(bb1, c_bb1, B1), (bb2, c_bb2, 1), (tb0, c_t0, O0), (tb1, c_t1, O1),
                   (tb2, c_t2, O2), (tb3, c_t3, O3)]
        N_VEC = c_w4 + O3

        def rhs_of(g):
            return feat[:, SG * g:SG * g + SG, 1:NF]

        def lhs_of(g):
            return feat[:, SG * g:SG * g + SG, :].rearrange("p s n -> p (s n)")[:, 0:NP * (SG - 1) + NN]

        def piece_bank(q):
            return bank[6 + q % 2]

        def flat(ap):
            return ap.rearrange("p k n -> p (k n)")

        def half_bank(first, k):
            return bank[first + k // 2][:, C * (k % 2):C * (k % 2) + C]

        def dense_bank(j):
            return bank[(2, 3, 6, 7)[j]][0:NP, :]

        def b0_tile(c, k):
            pair = (bot0_even, bot0_odd)[c % 2]
            return half_bank(4 * (c % 2), k), pair[:, 0, k, :], pair[:, 1, k, :]

        def b0_bank(c, j):
            pair = (bot0_even, bot0_odd)[c % 2]
            hi, lo = (flat(pair[:, i, 2 * j:2 * j + 2, :]) for i in range(2))
            return bank[4 * (c % 2) + j][:, :], hi, lo

        def b1_tile(k):
            return half_bank(2, k), ringB_hi[:, k, :], ringB_lo[:, k, :]

        def h0_tile(k):
            return bank[(2, 3)[k] if k < 2 else 4 + k % 2][:, 0:C], ringA_hi[:, k % RA, :], ringA_lo[:, k % RA, :]

        def h1_tile(k):
            return half_bank(0, k), ringB_hi[:, k % RB, :], ringB_lo[:, k % RB, :]

        def h2_tile(k):
            hi, lo, slot = (ringA_hi, ringA_lo, 2 + k) if k < 2 else (ringB_hi, ringB_lo, k - 2)
            return half_bank(4, k), hi[:, slot, :], lo[:, slot, :]

        def h3_tile(k):
            slot = (2, 0)[k]
            return half_bank(0, k), ringB_hi[:, slot, :], ringB_lo[:, slot, :]

        def e_h0(k, first):
            return k + O3 if k >= 2 or first else k

        def e_h3(k, last):
            return k if last else k + 2

        E_H1, E_H2 = O3 + O0, O3 + O0 + O1

        def pieces_at(p, blocks, first):
            j = p // QB + (0 if first else 1)
            return [(p % QB, j)] if p // QB < blocks else []

        def pieces_l1(k, part, blocks, first):
            return pieces_at(4 * k + part, blocks, first) if k < 6 or first else []

        def pieces_l2(k, blocks, first):
            return pieces_at((4 if first else 3) * QB + k, blocks, first)

        def gram_half(t, j):
            return ((0, t + 1), (0, None), (1, t + 1), (1, None), (0, t + 2))[j]

        def x_steps(first):
            return (0, 5, 6, 7) if first else (0, 3, 4, 5)

        L1_PARTS = ((0, 2), (2, 4), (4, 6), (6, 8))

        EV0 = B1 * TILES

        def tr_cols(q):
            return (min(SL, TG * (q + 1)) - TG * q) * P

        def transposed(ps, q):
            return ps[:, 0:tr_cols(q)].rearrange("p (f b) -> p f b", b=BS)

        def feat_of(q):
            f = 1 + 2 * TG * q
            return feat[:, :, f:f + tr_cols(q) // BS].rearrange("p b f -> p f b")

        def gram_part(ps, s):
            return ps[NP * s:NP * s + NN, 0:GG * NN * SG].rearrange(
                "p (g s m) -> p m g s", g=GG, s=SG)[:, :, :, s]

        def gram_dst(half, blk, q, s):
            b0 = BS * (blk % 2) + GG * SG * q
            v = gram[NP * half:NP * half + NN, :, b0:b0 + GG * SG]
            return v.rearrange("p m (g s) -> p m g s", s=SG)[:, :, :, s]

        def tw0_split(k):
            kk = KROWS[k]
            return (s_tw0[k], 16 * sum(run[0] == k for run in w0_runs),
                    w01_raw[0:kk, k, :], w01_hi[0:kk, k, :], w01_lo[0:kk, k, :])

        def tw1_splits(j):
            return [(s_tw1[j], 16, w01_raw[:, KX + k, :], w01_hi[:, KX + k, :], w01_lo[:, KX + k, :])
                    for k in (2 * j, 2 * j + 1)]

        splits = [tw0_split(0)] + tw1_splits(0) + [tw0_split(1)] + tw1_splits(1) + [tw0_split(2)] + \
            tw1_splits(2) + tw1_splits(3) + [(s_tw3, 16, flat(w3_raw[:, :, :]), flat(w3_hi[:, :, :]),
                                              flat(w3_lo[:, :, :])), tw0_split(3)]
        N_EARLY = len(splits)
        for j in range(0, O1, 2):
            splits.append((s_tw2[j // 4], 16, flat(w2_raw[:, j:j + 2, :]), flat(w2_hi[:, j:j + 2, :]),
                           flat(w2_lo[:, j:j + 2, :])))
        LOAD_GAP = len(w0_runs) // 4
        N_SMALL = 3

        PLACES = 3 * QB // 4

        def step_pieces(c, place):
            return (PLACES * (c - 2) + place,) if 2 <= c < 6 else ()

        BLOCK3_PIECES = range(3 * QB, 4 * QB)

        def step_splits(c, place):
            n = 2 * (c - 1) + place
            return (n,) if 0 <= n < N_EARLY else ()

        assert 2 * (TILES - 1) >= N_EARLY

        block = ctx.enter_context(nc.Block())

        @block.sync
        def _(sp):
            def load_indices(part, k0, k1):
                for j in range(2):
                    sp.dma_start(raw_idx[BS * j:BS * j + BS, k0:k1, :],
                                 sparse[BS * k0:BS * k1, :].rearrange("(k s) t -> s k t", s=BS)
                                 ).then_inc(s_idx[part], 16)

            def load_ktiles(dst, w, k0, k1, done):
                sp.dma_start(dst, w[P * k0:P * k1, :].rearrange("(k p) n -> p k n", p=P)
                             ).then_inc(done, 16)

            load_indices(0, 0, 4)
            sp.dma_start(dense_rows[:, :, 0:ND], dense.rearrange("(c p) k -> p c k", p=P)).then_inc(s_dense, 16)
            sp.dma_start(bw0_raw[0:ND, :], bw0).then_inc(s_bw[0], 16)
            sp.dma_start(bw0_raw[ND:ND + 1, :], bb0.rearrange("(a n) -> a n", a=1)).then_inc(s_bw[0], 16)
            load_ktiles(bw1_raw[:, :, :], bw1, 0, B0, s_bw[1])
            for v, c, n in vectors:
                sp.dma_start(vec_rows[c:c + n, :], v.rearrange("(j p) -> j p", p=P)).then_inc(s_vec, 16)
            sp.dma_start(vec_rows[c_w4:c_w4 + O3, :], tw4.rearrange("(j p) a -> j (p a)", p=P)).then_inc(s_vec, 16)
            load_ktiles(bw2_raw[:, :, :], bw2, 0, B1, s_bw[2])
            load_indices(1, 4, BLOCKS)
            for i, (k, p0, row, cnt) in enumerate(w0_runs):
                sp.dma_start(w01_raw[p0:p0 + cnt, k, :], tw0[row:row + cnt, :]).then_inc(s_tw0[k], 16)
                if i % LOAD_GAP == 0 and i // LOAD_GAP < 4:
                    j = i // LOAD_GAP
                    load_ktiles(w01_raw[:, KX + 2 * j:KX + 2 * j + 2, :], tw1, 2 * j, 2 * j + 2, s_tw1[j])
            load_ktiles(w3_raw[:, :, :], tw3, 0, O2, s_tw3)
            sp.dma_start(b4[:, :], bass.AP(tb4.tensor, 0, [[0, P], [1, 1]])).then_inc(s_b4, 16)

            def move_pairs(t, h, first=False):
                sp.wait_ge(a_gr, QG * (4 * t + 2 * h + 2))
                sp.wait_ge(v_gr, QG * (4 * t + 2 * h + 2))
                if not first:
                    for k in range(1, KX):
                        sp.wait_ge(v_x[k], t)
                sp.dma_start(gram_dram[h], gram[NP * h:NP * h + NN, :, :]).then_inc(s_gram[h], 16)
                sp.wait_ge(s_gram[h], 16 * t + 16)
                for k, tile in enumerate(rectangles):
                    p0 = 0
                    for n0, m0, slope, nr, ncols in tile:
                        src = bass.AP(gram_dram.tensor, ((h * NN + n0) * NN + m0 - 1) * HALF,
                                      [[(R * (NN + 1) if slope else NN) * HALF, nr], [HALF, ncols], [1, HALF]])
                        p1 = p0 + nr * ncols
                        sp.dma_start(pair_rows[p0:p1, k, HALF * h:HALF * h + HALF], src
                                     ).then_inc(s_pairs[k][h], 16)
                        p0 = p1

            move_pairs(0, 0, True)
            move_pairs(0, 1, True)
            sp.wait_ge(p_b2, TILES)
            for j in range(2):
                load_ktiles(w2_raw[:, 4 * j:4 * j + 4, :], tw2, 4 * j, 4 * j + 4, s_tw2[j])
            with sp.Fori(1, TILES) as t:
                move_pairs(t, 0)
                move_pairs(t, 1)
            sp.wait_ge(v_zt, 1)
            sp.dma_start(out.rearrange("(c p) -> c p", p=P), act_f32[0:B // P, 0, 0:P]).then_inc(s_out, 16)
            sp.wait_ge(s_out, 16)

        @block.gpsimd
        def _(gp):
            gp.iota(table_base[:, :], pattern=[[V, NT]], base=0, channel_multiplier=0).then_inc(g_const, 1)
            gp.memset(ident[:, :], 0.0).then_inc(g_const, 1)
            gp.wait_ge(g_const, 2)
            gp.affine_select(out=ident[:, :], in_=ident[:, :], compare_op=ALU.not_equal, fill=1.0, base=0,
                             pattern=[[-1, P]], channel_multiplier=1).then_inc(g_const, 1)

            def gather(i):
                for u in range(SL):
                    gp.indirect_dma_start(rows[i % 2][:, u, :], None, table_rows,
                                          bass.IndirectOffsetOnAxis(ap=idx_cur[:, i, u:u + 1], axis=0)
                                          ).then_inc(s_rows[i % 2], 16)

            gp.wait_ge(v_idx0, 1)
            for i in range(4):
                if i >= 2:
                    gp.wait_ge(p_tr, QT * (i - 1))
                gather(i)
            with gp.Fori(1, TILES) as t:
                for i in range(4):
                    gp.wait_ge(v_idx, 4 * t + i - 3)
                    gp.wait_ge(p_tr, QT * (4 * t + i - 1))
                    gp.sem_inc(g_block, 1)
                    gather(i)

        @block.scalar
        def _(act):
            def split_hi(loaded, count, raw, hi, _):
                act.wait_ge(loaded, count)
                act.activation(hi, raw, ACT.Copy).then_inc(a_split, 1)

            def layer_hi(count, tile, col, slot):
                ps, hi, _ = tile
                if not (isinstance(count, int) and count < 2):
                    act.wait_ge(v_ev, count - 1)
                act.activation(act_f32[:, slot, :], ps, ACT.Relu, bias=bias[:, col:col + 1])
                act.activation(hi, ps, ACT.Relu, bias=bias[:, col:col + 1]).then_inc(a_ev, 1)

            def bottom0(c):
                for j in range(B0 // 2):
                    act.wait_ge(p_b0, B0 * c + 2 * j + 2)
                    ps, hi, _ = b0_bank(c, j)
                    act.activation(hi, ps, ACT.Relu).then_inc(a_b0, 1)

            def bottom1(c, k):
                act.wait_ge(p_b1, B1 * c + B1)
                layer_hi(B1 * c + k, b1_tile(k), c_bb1 + k, k % 2)

            def piece(q, b, half, blk, gram_done):
                ps = piece_bank(q)
                if q < QT:
                    if q % 2 == 0:
                        act.wait_ge(p_tr, QT * b + q + 1)
                        act.activation(feat_of(q), transposed(ps, q), ACT.Copy).then_inc(a_tr, 1)
                    return
                if q == QT and gram_done is not None:
                    act.wait_ge(s_gram[half], 16 * gram_done)
                act.wait_ge(p_gr, QG * b + q - QT + 1)
                act.activation(gram_dst(half, blk, q - QT, 0), gram_part(ps, 0), ACT.Copy)
                act.activation(gram_dst(half, blk, q - QT, 1), gram_part(ps, 1), ACT.Copy).then_inc(a_gr, 1)

            def early_piece(p):
                b = p // QB
                piece(p % QB, b, b // 2, b, None)

            def split_x(t, k):
                if k == 0:
                    act.wait_ge(p_l0, O0 * t)
                    src = dense_out[:, bass.ds(t * C, C)]
                else:
                    for h in range(2):
                        act.wait_ge(s_pairs[k - 1][h], 16 * len(rectangles[k - 1]) * (t + 1))
                    src = pair_rows[0:KROWS[k], k - 1, :]
                act.activation(x_hi[0:KROWS[k], k, :], src, ACT.Copy).then_inc(a_x, 1)

            def dense_hi(j):
                act.wait_ge(p_pre, 1 + j)
                act.activation(dense_T[0:NP, 512 * j:512 * j + 512], dense_bank(j), ACT.Copy)
                act.activation(dense_T[2 * NP:3 * NP, 512 * j:512 * j + 512], dense_bank(j), ACT.Copy
                               ).then_inc(a_pre, 1)

            act.wait_ge(v_one, 1)
            act.activation(act_f32[:, 0, 0:B // P], dense_rows[:, :, ND], ACT.Relu)
            act.wait_ge(v_zero, 1)
            act.wait_ge(s_bw[0], 32)
            act.activation(bw0s[0:ND + 1, :], bw0_raw[0:ND + 1, :], ACT.Copy)
            act.activation(bw0s[32:32 + ND + 1, :], bw0_raw[0:ND + 1, :], ACT.Copy).then_inc(a_split, 1)
            dense_hi(0)
            split_hi(s_bw[1], 16, flat(bw1_raw[:, :, :]), flat(bw1_hi[:, :, :]), flat(bw1_lo[:, :, :]))

            def at(c, place):
                for p in step_pieces(c, place):
                    early_piece(p)

            def split_at(c, place):
                for n in step_splits(c, place):
                    split_hi(*splits[n])

            bottom0(0)
            for c in range(TILES):
                if c == 6:
                    for p in BLOCK3_PIECES:
                        early_piece(p)
                if c + 1 < TILES:
                    bottom0(c + 1)
                if c == 0:
                    dense_hi(1)
                    split_hi(s_bw[2], 16, flat(bw2_raw[:, :, :]), flat(bw2_hi[:, :, :]), flat(bw2_lo[:, :, :]))
                    act.wait_ge(v_bias, 1)
                if c == 1:
                    dense_hi(2)
                    dense_hi(3)
                at(c, 0)
                split_at(c, 0)
                at(c, 1)
                at(c, 2)
                split_at(c, 1)
                bottom1(c, 0)
                at(c, 3)
                bottom1(c, 1)
                at(c, 4)
                at(c, 5)
            act.wait_ge(v_dense, TILES)
            for k in range(KX):
                split_x(0, k)

            def h3(t, last):
                for k in range(O3):
                    act.wait_ge(p_l3, O3 * t + O3)
                    e = e_h3(k, last)
                    layer_hi(EV * (t + 1) + EV0 - O3 + e, h3_tile(k), c_t3 + k, e % 2)

            def tile(t, blocks, first=False):
                def layer(e, tile, col):
                    layer_hi(EV * t + EV0 - O3 + e, tile, col, e % 2)

                def h0(k):
                    act.wait_ge(p_l0, O0 * t + k + 1)
                    if k >= RA:
                        act.wait_ge(p_k1, O0 * t + k - RA + 1)
                    layer(e_h0(k, first), h0_tile(k), c_t0 + k)

                def h1(k):
                    act.wait_ge(p_l1, O1 * t + (k | 1) + 1)
                    if k >= RB:
                        act.wait_ge(p_k2, O1 * t + k - RB + 1)
                    layer(E_H1 + k, h1_tile(k), c_t1 + k)

                def pc(places):
                    for q, j in places:
                        half, done = gram_half(t, j)
                        piece(q, 4 * t + 4 + j, half, j, done)

                h0(0)
                h0(1)
                pc(pieces_l1(0, 0, blocks, first))
                if not first:
                    h3(t - 1, False)
                h0(2)
                for k in range(O0):
                    if k + 3 < O0:
                        h0(k + 3)
                    for part in range(1 if k == 0 else 0, 4):
                        pc(pieces_l1(k, part, blocks, first))
                        if k == O0 - 1 and part in (1, 2):
                            h1(part - 1)
                    if first and 1 <= k <= len(splits) - N_EARLY:
                        split_hi(*splits[N_EARLY + k - 1])
                for k in range(O1):
                    if k + 2 < O1:
                        h1(k + 2)
                    if k < O1 - 1:
                        pc(pieces_l2(k, blocks, first))
                    if blocks and k in x_steps(first):
                        split_x(t + 1, x_steps(first).index(k))
                for k in range(O2):
                    act.wait_ge(p_l2, O2 * t + (k | 1) + 1)
                    layer(E_H2 + k, h2_tile(k), c_t2 + k)
                pc(pieces_l2(O1 - 1, blocks, first))

            tile(0, 5, True)
            with act.Fori(1, TILES - 2) as t:
                tile(t, 4)
            tile(TILES - 2, 3)
            tile(TILES - 1, 0)
            h3(TILES - 1, True)

        @block.vector
        def _(dve):
            def make_indices(part, k0, k1, step):
                dve.wait_ge(s_idx[part], 32)
                dve.tensor_scalar(wrap[:, k0:k1, :], raw_idx[:, k0:k1, :], 0.0, float(V), ALU.is_lt, ALU.mult
                                  ).then_inc(v_i, 1)
                dve.wait_ge(v_i, step + 1)
                dve.tensor_tensor(wrapped[:, k0:k1, :], raw_idx[:, k0:k1, :], wrap[:, k0:k1, :], ALU.add
                                  ).then_inc(v_i, 1)
                dve.wait_ge(v_i, step + 2)
                dve.tensor_scalar(clamped[:, k0:k1, :], wrapped[:, k0:k1, :], 0.0, float(V - 1), ALU.max, ALU.min
                                  ).then_inc(v_i, 1)
                dve.wait_ge(v_i, step + 3)
                for j in range(2):
                    h = slice(BS * j, BS * j + BS)
                    src = clamped[h, k0:k1, :].rearrange("p k (u j) -> p k u j", j=2)[:, :, :, j]
                    base = table_base[h, :].rearrange("p (u j) -> p u j", j=2)[:, :, j].rearrange(
                        "p (a u) -> p a u", a=1).to_broadcast([BS, k1 - k0, SL])
                    last = dve.tensor_tensor(idx_all[h, k0:k1, :], src, base, ALU.add)
                last.then_inc(v_i, 1)
                dve.wait_ge(v_i, step + 4)

            dve.memset(dense_rows[:, :, ND:ND + 1], 1.0).then_inc(v_one, 1)
            dve.memset(dense_rows[:, :, ND + 1:NP], 0.0).then_inc(v_one, 1)
            dve.memset(bw0s[:, :].bitcast(F32), 0.0).then_inc(v_zero, 1)
            dve.memset(feat[:, :, NF:NP], 0.0).then_inc(v_zero, 1)
            dve.memset(idx_all[:, BLOCKS, :], 0)
            dve.memset(z[:, :], 0.0).then_inc(v_z, 1)
            dve.wait_ge(g_const, 1)
            make_indices(0, 0, 4, 0)
            dve.tensor_copy(idx_cur[:, :, :], idx_all[:, 0:4, :]).then_inc(v_idx0, 1)

            def split_lo(n, raw, hi, lo):
                dve.wait_ge(a_split, n + 1)
                dve.tensor_tensor(lo, raw, hi.bitcast(F32), ALU.subtract).then_inc(v_split, 1)

            dve.wait_ge(a_split, 1)
            dve.tensor_tensor(bw0s[64:64 + ND + 1, :], bw0_raw[0:ND + 1, :], bw0s[0:ND + 1, :].bitcast(F32),
                              ALU.subtract).then_inc(v_split, 1)

            def dense_lo(j):
                dve.wait_ge(a_pre, j + 1)
                dve.tensor_tensor(dense_T[NP:2 * NP, 512 * j:512 * j + 512], dense_bank(j),
                                  dense_T[0:NP, 512 * j:512 * j + 512].bitcast(F32), ALU.subtract).then_inc(v_pre, 1)

            dense_lo(0)
            split_lo(1, flat(bw1_raw[:, :, :]), flat(bw1_hi[:, :, :]), flat(bw1_lo[:, :, :]))

            def layer_lo(count, tile, slot):
                _, hi, lo = tile
                dve.wait_ge(a_ev, count + 1)
                dve.tensor_tensor(lo, act_f32[:, slot, :], hi.bitcast(F32), ALU.subtract).then_inc(v_ev, 1)

            def bottom0(c):
                for j in range(B0 // 2):
                    dve.wait_ge(a_b0, B0 // 2 * c + j + 1)
                    ps, hi, lo = b0_bank(c, j)
                    dve.scalar_tensor_tensor(lo, ps, 0.0, hi.bitcast(F32), ALU.max, ALU.subtract).then_inc(v_b0, 1)

            def bottom1(c):
                for k in range(B1):
                    layer_lo(B1 * c + k, b1_tile(k), k % 2)

            def bottom2(c):
                dve.wait_ge(p_b2, c + 1)
                dve.tensor_scalar(dense_out[:, C * c:C * c + C], bank[3][:, 0:C], bias[:, c_bb2:c_bb2 + 1], 0.0,
                                  ALU.add, ALU.max).then_inc(v_dense, 1)

            def piece(q, b, half, blk, gram_done, turn, refresh):
                ps = piece_bank(q)
                if q < QT:
                    if q % 2 == 0:
                        return
                    dve.wait_ge(p_tr, QT * b + q + 1)
                    if q == QT - 1:
                        dve.wait_ge(v_dense, b // 4 + 1 if isinstance(b, int) else TILES)
                        dve.tensor_copy(feat[:, :, 0], dense_out[:, bass.ds(b * BS, BS)])
                    dve.tensor_copy(feat_of(q), transposed(ps, q)).then_inc(v_tr, 1)
                    if q == QT - 1 and refresh:
                        dve.wait_ge(s_rows[blk % 2], 16 * SL * turn)
                        dve.tensor_copy(idx_cur[:, blk % 4, :], idx_all[:, bass.ds(b + 4, 1), :].rearrange(
                            "p a u -> p (a u)")).then_inc(v_idx, 1)
                else:
                    if q == QT and gram_done is not None:
                        dve.wait_ge(s_gram[half], 16 * gram_done)
                    dve.wait_ge(p_gr, QG * b + q - QT + 1)
                    dve.tensor_copy(gram_dst(half, blk, q - QT, 2), gram_part(ps, 2))
                    dve.tensor_copy(gram_dst(half, blk, q - QT, 3), gram_part(ps, 3)).then_inc(v_gr, 1)

            def early_piece(p):
                b = p // QB
                piece(p % QB, b, b // 2, b, None, b // 2 + 1, True)

            def split_x(t, k):
                dve.wait_ge(a_x, KX * t + k + 1)
                src = pair_rows[0:KROWS[k], k - 1, :] if k else dense_out[:, bass.ds(t * C, C)]
                dve.tensor_tensor(x_lo[0:KROWS[k], k, :], src, x_hi[0:KROWS[k], k, :].bitcast(F32),
                                  ALU.subtract).then_inc(v_x[k], 1)

            def at(c, place):
                for p in step_pieces(c, place):
                    early_piece(p)

            def split_at(c, place):
                for n in step_splits(c, place):
                    split_lo(N_SMALL + n, *splits[n][2:])

            bottom0(0)
            dve.wait_ge(p_pre, 5)
            dve.tensor_copy(bias[:, 0:N_VEC], bank[5][:, 0:N_VEC]).then_inc(v_bias, 1)
            for c in range(TILES):
                if c == 6:
                    for p in BLOCK3_PIECES:
                        early_piece(p)
                if c + 1 < TILES:
                    bottom0(c + 1)
                if c == 0:
                    dense_lo(1)
                    split_lo(2, flat(bw2_raw[:, :, :]), flat(bw2_hi[:, :, :]), flat(bw2_lo[:, :, :]))
                    make_indices(1, 4, BLOCKS, 4)
                at(c, 0)
                if c > 0:
                    bottom2(c - 1)
                if c == 1:
                    dense_lo(2)
                    dense_lo(3)
                split_at(c, 0)
                at(c, 1)
                at(c, 2)
                split_at(c, 1)
                at(c, 3)
                bottom1(c)
                at(c, 4)
                at(c, 5)
            bottom2(TILES - 1)
            dve.wait_ge(v_bias, 1)
            dve.tensor_copy(w4[:, :, 0], bias[:, c_w4:c_w4 + O3]).then_inc(v_w4, 1)
            dve.wait_ge(v_w4, 1)
            dve.tensor_tensor(w4[:, :, 1], bias[:, c_w4:c_w4 + O3], w4[:, :, 0].bitcast(F32), ALU.subtract
                              ).then_inc(v_w4, 1)
            for k in range(KX):
                split_x(0, k)

            def h3(t, last):
                for k in range(O3):
                    e = e_h3(k, last)
                    layer_lo(EV * (t + 1) + EV0 - O3 + e, h3_tile(k), e % 2)

            def score(t):
                dve.wait_ge(p_l4, t + 1)
                dve.tensor_reduce(z[:, :], bank[2][:, C:C + 4].rearrange("p (j w) -> p j w", w=2), AX.X, ALU.add
                                  ).then_inc(v_zs, 1)
                dve.wait_ge(v_zs, t + 1)
                dve.tensor_scalar(z_all[:, bass.ds(2 * t, 2)], z[:, :], b4[:, 0:1], 0.0, ALU.add, ALU.max
                                  ).then_inc(v_z, 1)

            def tile(t, blocks, first=False):
                def layer(e, tile):
                    layer_lo(EV * t + EV0 - O3 + e, tile, e % 2)

                def pc(places):
                    for q, j in places:
                        half, done = gram_half(t, j)
                        piece(q, 4 * t + 4 + j, half, j, done, 2 * t + 3 + j // 2, blocks >= 4)

                layer(e_h0(0, first), h0_tile(0))
                layer(e_h0(1, first), h0_tile(1))
                pc(pieces_l1(0, 0, blocks, first))
                if not first:
                    h3(t - 1, False)
                layer(e_h0(2, first), h0_tile(2))
                for k in range(O0):
                    if k + 3 < O0:
                        layer(e_h0(k + 3, first), h0_tile(k + 3))
                    if k == 0 and not first:
                        score(t - 1)
                    for part in range(1 if k == 0 else 0, 4):
                        pc(pieces_l1(k, part, blocks, first))
                        if k == O0 - 1 and part in (1, 2):
                            layer(E_H1 + part - 1, h1_tile(part - 1))
                    if first and 1 <= k <= len(splits) - N_EARLY:
                        n = N_EARLY + k - 1
                        split_lo(N_SMALL + n, *splits[n][2:])
                for k in range(O1):
                    if k + 2 < O1:
                        layer(E_H1 + k + 2, h1_tile(k + 2))
                    if k < O1 - 1:
                        pc(pieces_l2(k, blocks, first))
                    if blocks and k in x_steps(first):
                        split_x(t + 1, x_steps(first).index(k))
                for k in range(O2):
                    layer(E_H2 + k, h2_tile(k))
                pc(pieces_l2(O1 - 1, blocks, first))

            dve.wait_ge(s_b4, 16)
            tile(0, 5, True)
            with dve.Fori(1, TILES - 2) as t:
                tile(t, 4)
            tile(TILES - 2, 3)
            tile(TILES - 1, 0)
            h3(TILES - 1, True)
            score(TILES - 1)
            dve.wait_ge(p_z, 1)
            dve.tensor_copy(act_f32[0:B // P, 0, 0:P], bank[2][0:B // P, 0:P]).then_inc(v_zt, 1)

        @block.tensor
        def _(pe):
            def mm3(ps, w_hi, w_lo, r_hi, r_lo, first, last):
                pe.matmul(ps, w_hi, r_hi, start=first, stop=False, skip_group_check=True)
                pe.matmul(ps, w_hi, r_lo, start=False, stop=False, skip_group_check=True)
                return pe.matmul(ps, w_lo, r_hi, start=False, stop=last, skip_group_check=True)

            def piece(q, b, par, turn):
                ps = piece_bank(q)
                if q < QT:
                    if q == 0:
                        pe.wait_ge(s_rows[par], 16 * SL * turn)
                    for u in range(TG * q, min(SL, TG * q + TG)):
                        last = pe.transpose(ps[:, (u % TG) * P:(u % TG) * P + P], rows[par][:, u, :], ident[:, :])
                    last.then_inc(p_tr, 1)
                else:
                    if q == QT:
                        pe.wait_ge(a_tr, QT // 2 * (b + 1))
                        pe.wait_ge(v_tr, QT // 2 * (b + 1))
                    for gi in range(GG):
                        g = GG * (q - QT) + gi
                        o = ps[:, gi * NN * SG:(gi + 1) * NN * SG]
                        last = pe.matmul(o[0:NP * (SG - 1) + NN, :], lhs_of(g), rhs_of(g), start=True, stop=True)
                    last.then_inc(p_gr, 1)

            def bank_free(q, b):
                q, b = (q - 2, b) if q >= 2 else (q + QB - 2, b - 1)
                if isinstance(b, int) and b < 0:
                    return
                if q < QT:
                    pe.wait_ge((a_tr, v_tr)[q % 2], QT // 2 * b + q // 2 + 1)
                else:
                    pe.wait_ge(a_gr, QG * b + q - QT + 1)
                    pe.wait_ge(v_gr, QG * b + q - QT + 1)

            pe.wait_ge(g_const, 3)
            pe.wait_ge(s_dense, 16)
            pe.wait_ge(v_one, 2)

            def dense_group(j):
                for c in range(4):
                    last = pe.transpose(dense_bank(j)[:, P * c:P * c + P], dense_rows[:, 4 * j + c, :], ident[:, :])
                last.then_inc(p_pre, 1)

            dense_group(0)
            dense_group(1)

            def bottom0(c):
                pe.wait_ge(v_pre, c // 2 + 1)
                if c == 1:
                    pe.wait_ge(v_bias, 1)
                if c >= 2:
                    pe.wait_ge(v_b0, B0 // 2 * (c - 1))
                for k in range(B0):
                    pe.matmul(b0_tile(c, k)[0], bw0s[:, P * k:P * k + P], dense_T[:, C * c:C * c + C],
                              start=True, stop=True).then_inc(p_b0, 1)

            def bottom1(c, o):
                for k in range(B0):
                    if o == 0:
                        pe.wait_ge(v_b0, B0 // 2 * c + k // 2 + 1)
                    _, r_hi, r_lo = b0_tile(c, k)
                    last = mm3(b1_tile(o)[0], bw1_hi[:, k, P * o:P * o + P], bw1_lo[:, k, P * o:P * o + P],
                               r_hi, r_lo, k == 0, k == B0 - 1)
                last.then_inc(p_b1, 1)

            def bottom2(c):
                if c > 0:
                    pe.wait_ge(v_dense, c)
                for k in range(B1):
                    pe.wait_ge(v_ev, B1 * c + k + 1)
                    last = mm3(bank[3][:, 0:C], bw2_hi[:, k, :], bw2_lo[:, k, :], ringB_hi[:, k, :],
                               ringB_lo[:, k, :], k == 0, k == B1 - 1)
                last.then_inc(p_b2, 1)

            def early_piece(p):
                b, q = divmod(p, QB)
                if p == 0:
                    pe.wait_ge(v_pre, 4)
                    pe.wait_ge(v_zero, 2)
                bank_free(q, b)
                piece(q, b, b % 2, b // 2 + 1)

            def at(c, place):
                for p in step_pieces(c, place):
                    early_piece(p)

            pe.wait_ge(v_split, 1)
            bottom0(0)
            dense_group(2)
            dense_group(3)
            pe.wait_ge(s_vec, 16 * (len(vectors) + 1))
            pe.transpose(bank[5][:, 0:N_VEC], vec_rows[0:N_VEC, :], ident[0:N_VEC, 0:N_VEC]).then_inc(p_pre, 1)
            for c in range(TILES):
                if c == 6:
                    for p in BLOCK3_PIECES:
                        early_piece(p)
                if c + 1 < TILES:
                    bottom0(c + 1)
                at(c, 0)
                if c == 1:
                    pe.wait_ge(v_split, 3)
                if c > 0:
                    bottom2(c - 1)
                at(c, 1)
                if c == 0:
                    pe.wait_ge(v_split, 2)
                bottom1(c, 0)
                at(c, 2)
                bottom1(c, 1)
                at(c, 3)
                at(c, 4)
                at(c, 5)
            bottom2(TILES - 1)
            pe.wait_ge(v_split, N_SMALL + N_EARLY)
            pe.wait_ge(v_w4, 2)
            pe.wait_ge(v_dense, TILES)

            def tile(t, blocks, first=False):
                e = EV * t + EV0 - O3

                def pc(places):
                    for q, j in places:
                        bank_free(q, 4 * t + 4 + j)
                        piece(q, 4 * t + 4 + j, j % 2, 2 * t + 3 + j // 2)

                def layer0(o):
                    ps = h0_tile(o)[0]
                    if o >= 4:
                        pe.wait_ge(a_ev, e + e_h0(o - 2, first) + 1)
                    for k, kk in enumerate(KROWS):
                        if o == 0:
                            pe.wait_ge(v_x[k], t + 1)
                        last = mm3(ps, w01_hi[0:kk, k, P * o:P * o + P],
                                   w01_lo[0:kk, k, P * o:P * o + P], x_hi[0:kk, k, :], x_lo[0:kk, k, :],
                                   k == 0, k == KX - 1)
                    last.then_inc(p_l0, 1)

                def layer1(k, o0, o1):
                    if o0 == 0:
                        pe.wait_ge(v_ev, e + e_h0(k, first) + 1)
                    for o in range(o0, o1):
                        if k == 0 and o == 4:
                            pe.wait_ge(v_z, t + 1)
                        if k == 0 and o == 6:
                            pe.wait_ge(a_ev, e + e_h0(1, first) + 1)
                        _, r_hi, r_lo = h0_tile(k)
                        last = mm3(h1_tile(o)[0],
                                   w01_hi[:, KX + k, P * o:P * o + P], w01_lo[:, KX + k, P * o:P * o + P],
                                   r_hi, r_lo, k == 0 and o % 2 == 0, k == O0 - 1)
                        if k == O0 - 1:
                            last.then_inc(p_l1, 1)
                    if o1 == O1 and k < O0 - 1:
                        last.then_inc(p_k1, 1)
                    elif o1 == O1:
                        pe.nop().then_inc(p_k1, 1)

                def layer2(k):
                    pe.wait_ge(v_ev, e + E_H1 + k + 1)
                    _, r_hi, r_lo = h1_tile(k)
                    for o in range(O2):
                        last = mm3(h2_tile(o)[0], w2_hi[:, k, P * o:P * o + P],
                                   w2_lo[:, k, P * o:P * o + P], r_hi, r_lo,
                                   k == 0 and o % 2 == 0, k == O1 - 1)
                        if k == O1 - 1:
                            last.then_inc(p_l2, 1)
                    if k < O1 - 1:
                        last.then_inc(p_k2, 1)
                    else:
                        pe.nop().then_inc(p_k2, 1)

                layer0(0)
                layer0(1)
                pc(pieces_l1(0, 0, blocks, first))
                if not first:
                    layer3(t - 1)
                layer0(2)
                for k in range(O0):
                    if k + 3 < O0:
                        layer0(k + 3)
                    if k == 0 and not first:
                        layer4(t - 1, False)
                    for part, (o0, o1) in enumerate(L1_PARTS):
                        layer1(k, o0, o1)
                        if k > 0 or part > 0:
                            pc(pieces_l1(k, part, blocks, first))
                for k in range(O1):
                    if first:
                        pe.wait_ge(v_split, N_SMALL + N_EARLY + k // 2 + 1)
                    layer2(k)
                    pc(pieces_l2(k, blocks, first))

            def layer3(t):
                for k in range(O2):
                    pe.wait_ge(v_ev, EV * t + EV0 - O3 + E_H2 + k + 1)
                    _, r_hi, r_lo = h2_tile(k)
                    for o in range(O3):
                        last = mm3(h3_tile(o)[0], w3_hi[:, k, P * o:P * o + P],
                                   w3_lo[:, k, P * o:P * o + P], r_hi, r_lo,
                                   k == 0 and o == 0, k == O2 - 1)
                        if k == O2 - 1:
                            last.then_inc(p_l3, 1)

            def layer4(t, last_pass):
                pe.wait_ge(v_ev, EV * (t + 1) + EV0 - O3 + e_h3(O3 - 1, last_pass) + 1)
                for j in range(2):
                    for k in range(O3):
                        for s, h in enumerate(h3_tile(k)[1:]):
                            last = pe.matmul(bank[2][:, C + 2 * j:C + 2 * j + 2], h[:, P * j:P * j + P], w4[:, k, :],
                                             start=(k == 0 and s == 0), stop=(k == O3 - 1 and s == 1),
                                             skip_group_check=True)
                last.then_inc(p_l4, 1)

            tile(0, 5, True)
            with pe.Fori(1, TILES - 2) as t:
                tile(t, 4)
            tile(TILES - 2, 3)
            tile(TILES - 1, 0)
            layer3(TILES - 1)
            layer4(TILES - 1, True)
            pe.wait_ge(v_z, TILES + 1)
            pe.transpose(bank[2][0:B // P, 0:P], z_all[:, :], ident[:, :]).then_inc(p_z, 1)


_NAMES = ["r_dense", "r_sparse", "L0_rec_emb_tables", "L0_rec_bw0", "L0_rec_bb0", "L0_rec_bw1", "L0_rec_bb1",
          "L0_rec_bw2", "L0_rec_bb2", "L0_rec_tw0", "L0_rec_tb0", "L0_rec_tw1", "L0_rec_tb1", "L0_rec_tw2",
          "L0_rec_tb2", "L0_rec_tw3", "L0_rec_tb3", "L0_rec_tw4", "L0_rec_tb4"]


def kernel(**inputs):
    import numpy as np
    import concourse.bacc as bacc
    from concourse.bass_utils import run_bass_kernel_spmd

    nc = bacc.Bacc("TRN2", target_bir_lowering=False, num_devices=1)
    arrays, args = {}, []
    for name in _NAMES:
        a = np.ascontiguousarray(inputs[name])
        arrays[name + "_in"] = a
        args.append(nc.dram_tensor(name + "_in", a.shape, mybir.dt.from_np(a.dtype), kind="ExternalInput").ap())
    out = nc.dram_tensor("scores_out", (inputs["r_dense"].shape[0],), F32, kind="ExternalOutput").ap()
    dlrm(nc, *args, out)
    result = run_bass_kernel_spmd(nc, [arrays], core_ids=[0])
    return result.results[0]["scores_out"]
```
